# Optimizing a Trainium2 kernel written in Bass

```python
import numpy as np
import jax
import jax.numpy as jnp

def _softmax(x, axis=-1):
    return jax.nn.softmax(x, axis=axis)

def _gelu(x):
    return jax.nn.gelu(x, approximate=True)

def _silu(x):
    return jax.nn.silu(x)

def _sigmoid(x):
    return jax.nn.sigmoid(x)

def _layernorm(x, axis=-1, eps=1e-05):
    m = jnp.mean(x, axis=axis, keepdims=True)
    v = jnp.var(x, axis=axis, keepdims=True)
    return (x - m) / jnp.sqrt(v + eps)

def _scatter_add(tgt, idx, src, axis=0):
    return tgt.at[idx].add(src)

def _segment_sum(src, seg, n):
    return jax.ops.segment_sum(src, seg, n)
kernel_name = 'mk_xattn_ffn_d1_seqx_r4_8f4130'

def setup_inputs(seed: int=0):
    np.random.seed(seed)
    _w = jnp.asarray

    def _rec_inputs():
        import jax
        import jax.numpy as jnp
        _rk = jax.random.key(seed)
        x = 0.0001212 + 1 * jax.random.normal(jax.random.fold_in(_rk, 1), (8, 256, 512), jnp.float32)
        _lenS = 256 - jax.random.randint(jax.random.fold_in(_rk, 7), (8,), 0, max(1, 256 // 4) + 1, jnp.int32)
        _lenS2 = 256 - jax.random.randint(jax.random.fold_in(_rk, 8), (8,), 0, max(1, 256 // 4) + 1, jnp.int32)
        _ctx_2048P = jax.random.normal(jax.random.fold_in(_rk, 11), (8, 16, 512), jnp.float32)
        _ctx_2048c = jax.random.dirichlet(jax.random.fold_in(_rk, 511), 0.3 * jnp.ones((16,), jnp.float32), (8, 256))
        _ctx_2048t = jnp.einsum('bsk,bkd->bsd', _ctx_2048c, _ctx_2048P)
        _ctx_2048t = _ctx_2048t * jax.lax.rsqrt(jnp.mean(jnp.square(_ctx_2048t)) + 1e-12) * 0.953939
        ctx_2048 = 0.000173663 + 1.0001 * (_ctx_2048t + 0.3 * jax.random.normal(jax.random.fold_in(_rk, 611), (8, 256, 512), jnp.float32))
        return (x, ctx_2048)
    x, ctx_2048 = _rec_inputs()

    def _L0_xattn_setup():
        import jax, jax.numpy as jnp
        import numpy as np
        B_DIM, T_DIM, C_DIM = (16, 256, 512)

        def _wkv(w, u, k, v):
            Bn, Tn, Cn = k.shape
            NEG_INF = jnp.float32(-1e+38)

            def step(carry, kv_t):
                p, q, o = carry
                kt, vt = kv_t
                no = jnp.maximum(o, u + kt)
                A = jnp.exp(o - no)
                E = jnp.exp(u + kt - no)
                y = (A * p + E * vt) / (A * q + E)
                no2 = jnp.maximum(w + o, kt)
                A2 = jnp.exp(w + o - no2)
                E2 = jnp.exp(kt - no2)
                return ((A2 * p + E2 * vt, A2 * q + E2, no2), y)
            init = (jnp.zeros((Bn, Cn), k.dtype), jnp.zeros((Bn, Cn), k.dtype), jnp.full((Bn, Cn), NEG_INF, k.dtype))
            kT = jnp.moveaxis(k, 1, 0)
            vT = jnp.moveaxis(v, 1, 0)
            _, yT = jax.lax.scan(step, init, (kT, vT))
            return jnp.moveaxis(yT, 0, 1)
        key = jax.random.key(seed)
        k1, k2, k3, k4 = jax.random.split(key, 4)
        w = -jnp.exp(jax.random.normal(k1, (C_DIM,), jnp.float32))
        u = jax.random.normal(k2, (C_DIM,), jnp.float32)
        k = jax.random.normal(k3, (B_DIM, T_DIM, C_DIM), jnp.float32)
        v = jax.random.normal(k4, (B_DIM, T_DIM, C_DIM), jnp.float32)
        return {'B': B_DIM, 'T': T_DIM, 'C': C_DIM, 'w': w, 'u': u, 'k': k, 'v': v}
    _L0_xattn_all = _L0_xattn_setup()
    _L0_xattn_in = {k: v for k, v in _L0_xattn_all.items() if k in ('w', 'u')}
    del _L0_xattn_all

    def _L0_ffn_setup():
        import jax, jax.numpy as jnp
        import numpy as np
        TOPK = 2
        N_EXPERTS = 8
        ROUTE_SCALE = 1.0
        key = jax.random.key(seed)
        ks = jax.random.split(key, 7)
        B, T, C = (4, 512, 512)
        H = 352
        HS = 704
        E = N_EXPERTS
        s = 0.02
        return {'x': jax.random.normal(ks[0], (B, T, C), jnp.float32), 'gate_w': jax.random.normal(ks[1], (E, C), jnp.float32) * s, 'gate_bias': jnp.zeros((E,), jnp.float32), 'shared_gw': jax.random.normal(ks[2], (2 * HS, C), jnp.float32) * s, 'shared_dw': jax.random.normal(ks[3], (C, HS), jnp.float32) * s, 'up_w': jax.random.normal(ks[4], (E, 2 * H, C), jnp.float32) * s, 'down_w': jax.random.normal(ks[5], (E, C, H), jnp.float32) * s}
    _L0_ffn_all = _L0_ffn_setup()
    _L0_ffn_in = {k: v for k, v in _L0_ffn_all.items() if k in ('gate_w', 'gate_bias', 'shared_gw', 'shared_dw', 'up_w', 'down_w')}
    del _L0_ffn_all
    return {'x': x, 'ctx_2048': ctx_2048, 'L0_xattn_w': _L0_xattn_in['w'], 'L0_xattn_u': _L0_xattn_in['u'], 'L0_ffn_gate_w': _L0_ffn_in['gate_w'], 'L0_ffn_gate_bias': _L0_ffn_in['gate_bias'], 'L0_ffn_shared_gw': _L0_ffn_in['shared_gw'], 'L0_ffn_shared_dw': _L0_ffn_in['shared_dw'], 'L0_ffn_up_w': _L0_ffn_in['up_w'], 'L0_ffn_down_w': _L0_ffn_in['down_w']}

def reference(x, ctx_2048, L0_xattn_w, L0_xattn_u, L0_ffn_gate_w, L0_ffn_gate_bias, L0_ffn_shared_gw, L0_ffn_shared_dw, L0_ffn_up_w, L0_ffn_down_w):
    import jax
    import jax.numpy as jnp

    def _L0_xattn_ref(B, T, C, w, u, k, v):
        import jax, jax.numpy as jnp
        import numpy as np
        B_DIM, T_DIM, C_DIM = (16, 256, 512)

        def _wkv(w, u, k, v):
            Bn, Tn, Cn = k.shape
            NEG_INF = jnp.float32(-1e+38)

            def step(carry, kv_t):
                p, q, o = carry
                kt, vt = kv_t
                no = jnp.maximum(o, u + kt)
                A = jnp.exp(o - no)
                E = jnp.exp(u + kt - no)
                y = (A * p + E * vt) / (A * q + E)
                no2 = jnp.maximum(w + o, kt)
                A2 = jnp.exp(w + o - no2)
                E2 = jnp.exp(kt - no2)
                return ((A2 * p + E2 * vt, A2 * q + E2, no2), y)
            init = (jnp.zeros((Bn, Cn), k.dtype), jnp.zeros((Bn, Cn), k.dtype), jnp.full((Bn, Cn), NEG_INF, k.dtype))
            kT = jnp.moveaxis(k, 1, 0)
            vT = jnp.moveaxis(v, 1, 0)
            _, yT = jax.lax.scan(step, init, (kT, vT))
            return jnp.moveaxis(yT, 0, 1)
        return _wkv(w, u, k, v)

    def _L0_ffn_ref(x, gate_w, gate_bias, shared_gw, shared_dw, up_w, down_w):
        import jax, jax.numpy as jnp
        import numpy as np
        TOPK = 2
        N_EXPERTS = 8
        ROUTE_SCALE = 1.0
        B, T, C = x.shape
        xf = x.reshape(-1, C)
        yg = xf @ shared_gw.T
        y, g = jnp.split(yg, 2, axis=-1)
        shared = jax.nn.silu(g) * y @ shared_dw.T
        scores = jax.nn.sigmoid(xf @ gate_w.T)
        _, topk_idx = jax.lax.top_k(scores + gate_bias, TOPK)
        w = jnp.take_along_axis(scores, topk_idx, axis=-1)
        w = w / jnp.sum(w, axis=-1, keepdims=True) * ROUTE_SCALE
        out = jnp.zeros_like(xf)
        for e in range(N_EXPERTS):
            we = jnp.sum(jnp.where(topk_idx == e, w, 0.0), axis=-1)
            gu = xf @ up_w[e].T
            g_e, u_e = jnp.split(gu, 2, axis=-1)
            h = jax.nn.silu(g_e) * u_e
            out = out + h @ down_w[e].T * we[:, None]
        return (shared + out).reshape(B, T, C)
    x = x + _L0_xattn_ref(8, 256, 512, L0_xattn_w, L0_xattn_u, _layernorm(x, axis=-1), ctx_2048)
    x = x + _L0_ffn_ref(_layernorm(x, axis=-1), L0_ffn_gate_w, L0_ffn_gate_bias, L0_ffn_shared_gw, L0_ffn_shared_dw, L0_ffn_up_w, L0_ffn_down_w)
    return x

_drawn_inputs = setup_inputs


def setup_inputs(seed=0):
    import zlib

    import numpy as np

    out = dict(_drawn_inputs(seed))
    spreads = {'L0_ffn_gate_bias': (0.0, 0.1)}
    factors = {}
    for name, (base, spread) in spreads.items():
        noise = np.random.default_rng([zlib.crc32(name.encode()), seed]).standard_normal(out[name].shape)
        drawn = base * np.exp(spread * noise) if base else spread * noise
        out[name] = jnp.asarray(drawn.astype(out[name].dtype))
    for name, factor in factors.items():
        out[name] = (out[name] * factor).astype(out[name].dtype)
    return out
```

```python
import concourse.bass as bass
from concourse import mybir
from contextlib import ExitStack

F32 = mybir.dt.float32
F32R = mybir.dt.float32r
BF16 = mybir.dt.bfloat16
FP16 = mybir.dt.float16
I32 = mybir.dt.int32
U32 = mybir.dt.uint32
ALU = mybir.AluOpType
ACT = mybir.ActivationFunctionType
AX = mybir.AxisListType

P = 128
B, T, C = 8, 256, 512
CT = C // P
TJ = T // P
TILES = B * TJ
E, TOPK = 8, 2
H = 352
HALVES = 2
HC = 3
UP = 2 * H
WCOLS = CT * UP + HC * C
DOWN0 = CT * UP
STEPS = TILES * TOPK + E - 1
STEPS_PAD = STEPS + 1
UNITS = HALVES + E
PER_BATCH = TJ * HALVES
EPS = 1e-5
R_CAP = 60.0


class Marks:

    def __init__(self, eng, sem):
        self.eng, self.sem, self.base, self.k = eng, sem, 0, 0

    def start(self, base):
        self.base, self.k = base, 0

    def mark(self, ins):
        self.k += 1
        ins.then_inc(self.sem, 1)
        return self.base + self.k

    def need(self, mark):
        self.eng.wait_ge(self.sem, mark)


def wait(eng, sem, value):
    if isinstance(value, int) and value <= 0:
        return
    eng.wait_ge(sem, value)


def cols(start, n):
    return slice(start, start + n) if isinstance(start, int) else bass.DynSlice(start, n)


def build(nc, x, ctx_t, w_row, wu_ch, gate_t, bias, weights, xn_dram, base_dram, ys_dram, out):
    with ExitStack() as ctx:
        def sb(name, shape, dt=F32):
            return ctx.enter_context(nc.sbuf_tensor(name, shape, dt))

        def pb(name, shape, dt=F32):
            return ctx.enter_context(nc.psum_tensor(name, shape, dt))

        def sem(name):
            return ctx.enter_context(nc.semaphore(name))

        w_hi = sb("w_hi", [P, HALVES, WCOLS], F32R)
        w_lo = sb("w_lo", [P, HALVES, WCOLS], F32R)
        w_raw = sb("w_raw", [P, 3 * WCOLS])
        ident = sb("ident", [P, P])
        ramp = sb("ramp", [P, T], F32R)
        neg_w = sb("neg_w", [P, C], F32R)
        iota_f = sb("iota_f", [P, T])
        row_id = sb("row_id", [P, 1])
        row_ii = sb("row_ii", [P, 1], I32)
        token_id = sb("token_id", [P, TILES])
        w_ch = sb("w_ch", [P, CT])
        u_ch = sb("u_ch", [P, CT])
        decay = sb("decay", [P, CT])
        u_first = sb("u_first", [P, CT])
        gate_hi = sb("gate_hi", [P, CT, E], F32R)
        gate_lo = sb("gate_lo", [P, CT, E], F32R)
        bias_sb = sb("bias_sb", [P, E])
        ones_b = sb("ones_b", [P, P], BF16)
        minus_half = sb("minus_half", [P, TJ])
        x_in = sb("x_in", [P, 2, TJ, C])
        v_in = sb("v_in", [P, 2, CT, T])
        k_tok = sb("k_tok", [P, TJ, C])
        stats = sb("stats", [P, 2, TJ, 6])
        moments = sb("moments", [P, 2, TJ, 2])
        rstd = sb("rstd", [P, 2, TJ])
        r_buf = sb("r_buf", [P, CT, T])
        e2 = sb("e2", [P, CT, T])
        ev = sb("ev", [P, CT, T])
        p_st = sb("p_st", [P, CT, T])
        q_st = sb("q_st", [P, CT, T])
        x1 = sb("x1", [P, 2, TJ, C])
        xn = sb("xn", [P, TJ, C])
        x_hi = sb("x_hi", [P, 2, TJ, CT, P], F32R)
        x_lo = sb("x_lo", [P, 2, TJ, CT, P], F32R)
        silu_g = sb("silu_g", [P, 2, H])
        h_sb = sb("h_sb", [P, 2, HC * P])
        h_hi = sb("h_hi", [P, 2, HC, P], F32R)
        h_lo = sb("h_lo", [P, 2, HC, P], F32R)
        score = sb("score", [P, TILES, E])
        top_i = sb("top_i", [P, TILES, 8], U32)
        top_f = sb("top_f", [P, TILES, TOPK])
        w_top = sb("w_top", [P, TILES, TOPK])
        w_sum = sb("w_sum", [P, TILES])
        w_tok = sb("w_tok", [P, TILES, TOPK])
        chosen_b = sb("chosen_b", [P, E * TILES], BF16)
        before_b = sb("before_b", [P, E * TILES], BF16)
        total_b = sb("total_b", [P, E], BF16)
        n_i = sb("n_i", [P, E], I32)
        n_tiles = sb("n_tiles", [P, E])
        ends = sb("ends", [P, E])
        starts = sb("starts", [P, E])
        ones8 = sb("ones8", [P, E])
        slot_f = sb("slot_f", [P, TILES, TOPK])
        slot_i = sb("slot_i", [P, TILES, TOPK], I32)
        part_i = sb("part_i", [P, 2, TILES, TOPK], I32)
        part_f = sb("part_f", [P, 2, TILES, TOPK])
        w_off = sb("w_off", [P, STEPS_PAD], I32)
        w_need = sb("w_need", [P, STEPS_PAD], I32)
        ends_i = sb("ends_i", [P, E], I32)
        idx_tab = sb("idx_tab", [P, STEPS_PAD], I32)
        spare_p = p_st.rearrange("p a t -> p (a t)")
        spare_q = q_st.rearrange("p a t -> p (a t)")
        onehot = spare_p[:, 0:256].rearrange("p (t k e) -> p t k e", t=TILES, k=TOPK)
        picked = spare_p[:, 256:512].rearrange("p (t k e) -> p t k e", t=TILES, k=TOPK)
        past = spare_p[:, 512:512 + (E - 1) * STEPS_PAD].rearrange("p (e s) -> p e s", e=E - 1)
        biased = spare_q[:, 0:128].rearrange("p (t e) -> p t e", t=TILES)
        top_v = spare_q[:, 128:256].rearrange("p (t e) -> p t e", t=TILES)
        chosen = spare_q[:, 256:384].rearrange("p (e t) -> p e t", e=E)
        upto = spare_q[:, 384:512].rearrange("p (e t) -> p e t", e=E)
        place = spare_q[:, 512:640].rearrange("p (e t) -> p e t", e=E)
        first0 = spare_q[:, 640:768].rearrange("p (e t) -> p e t", e=E)
        of_step = spare_p[:, 792:792 + STEPS_PAD]
        w_off_f = spare_p[:, 832:832 + STEPS_PAD]
        at_row = spare_q[:, 768:896].bitcast(FP16).rearrange("p (k r) -> p k r", k=TOPK)
        at_step = spare_q[:, 896:896 + STEPS_PAD].bitcast(FP16).rearrange("p (k s) -> p k s", k=TOPK)
        tri = spare_q[:, 936:1000].bitcast(BF16)
        wrow = x1[:, 1, 0, :]
        iota_i = x1[:, 1, 1, 0:T].bitcast(I32)
        gate_f = x1[:, 1, 1, T:T + CT * E].rearrange("p (a e) -> p a e", a=CT)
        idx_col = sb("idx_col", [P, 2], I32)
        y_idx = sb("y_idx", [P, 2, TOPK], I32)
        xg = [k_tok[:, j, :] for j in range(2)]
        xt = [r_buf[:, 2 * j:2 * j + 2, :].rearrange("p a t -> p (a t)") for j in range(2)]
        ht = [e2[:, 2 * j:2 * j + 2, :].rearrange("p a t -> p (a t)") for j in range(2)]
        ys = [ev[:, 2 * j:2 * j + 2, :].rearrange("p a t -> p (a t)") for j in range(2)]
        yg = [x_in[:, j, :, :] for j in range(2)]
        res = [x1[:, j, 0, :] for j in range(2)]
        acc = [x1[:, j, 1, :] for j in range(2)]

        ky = pb("ky", [P, 2, C])
        xt_ps = pb("xt_ps", [P, 2, C])
        g_ps = pb("g_ps", [P, C])
        u_ps = pb("u_ps", [P, C])
        ht_ps = pb("ht_ps", [P, C])
        d_ps = pb("d_ps", [P, C])
        logit_ps = ht_ps[:, HC * P:HC * P + TJ * E]
        rank_ps = xt_ps[:, 0, 0:E * TILES]
        count_ps = xt_ps[:, 0, E * TILES:E * TILES + E]
        table_ps = xt_ps[:, 1, 0:STEPS_PAD]

        const_in = sem("const_in")
        pool_mk = sem("pool_mk")
        dve_mk = sem("dve_mk")
        dve_passed = sem("dve_passed")
        pool_passed = sem("pool_passed")
        act_mk = sem("act_mk")
        x_dma = [sem(f"x_dma{s}") for s in range(2)]
        v_dma = [sem(f"v_dma{s}") for s in range(2)]
        xn_dma = sem("xn_dma")
        base_dma = [sem(f"base_dma{s}") for s in range(2)]
        raw_dma = sem("raw_dma")
        raw_ready = sem("raw_ready")
        pool_const = sem("pool_const")
        dve_const = sem("dve_const")
        split_hi = sem("split_hi")
        split_lo = sem("split_lo")
        var1_ready = sem("var1_ready")
        rstd1_ready = sem("rstd1_ready")
        ktok_ready = sem("ktok_ready")
        k_done = sem("k_done")
        e2_ready = sem("e2_ready")
        rarg_ready = sem("rarg_ready")
        r_ready = sem("r_ready")
        v_used = sem("v_used")
        y_ready = sem("y_ready")
        y_done = sem("y_done")
        var2_ready = sem("var2_ready")
        rstd2_ready = sem("rstd2_ready")
        xn_ready = sem("xn_ready")
        xt_done = sem("xt_done")
        xhi_ready = sem("xhi_ready")
        xlo_ready = sem("xlo_ready")
        logit_done = sem("logit_done")
        score_ready = sem("score_ready")
        g_done = sem("g_done")
        u_done = sem("u_done")
        silu_ready = sem("silu_ready")
        h_ready = sem("h_ready")
        ht_done = sem("ht_done")
        hhi_ready = sem("hhi_ready")
        hlo_ready = sem("hlo_ready")
        down_done = sem("down_done")
        base_ready = sem("base_ready")
        chosen_ready = sem("chosen_ready")
        rank_done = sem("rank_done")
        onehot_ready = sem("onehot_ready")
        onehot_used = sem("onehot_used")
        steps_ready = sem("steps_ready")
        idx_ready = sem("idx_ready")
        idx_set = sem("idx_set")
        xg_dma = [sem(f"xg_dma{s}") for s in range(2)]
        b_xt_done = sem("b_xt_done")
        b_xt_ready = sem("b_xt_ready")
        b_g_done = sem("b_g_done")
        b_u_done = sem("b_u_done")
        b_silu_ready = sem("b_silu_ready")
        b_h_ready = sem("b_h_ready")
        b_turn_done = sem("b_turn_done")
        b_ht_ready = sem("b_ht_ready")
        step_done = sem("step_done")
        ys_ready = sem("ys_ready")
        ys_dma = [sem(f"ys_dma{s}") for s in range(2)]
        yidx_set = sem("yidx_set")
        yg_dma = [[sem(f"yg_dma{s}{k}") for k in range(TOPK)] for s in range(2)]
        res_dma = [sem(f"res_dma{s}") for s in range(2)]
        part_ready = sem("part_ready")
        out_ready = sem("out_ready")
        out_dma = [sem(f"out_dma{s}") for s in range(2)]

        N_CONST = 6
        block = ctx.enter_context(nc.Block())

        @block.sync
        def _(sp):
            def load_x(b, k, s):
                sp.dma_start(x_in[:, s, :, :],
                             x[cols(b * T, T), :].rearrange("(j p) c -> p j c", p=P)).then_inc(x_dma[s], 16)

            def load_v(b, k, s):
                sp.dma_start(v_in[:, s, :, :],
                             ctx_t[cols(b * C, C), :].rearrange("(a p) t -> p a t", p=P)).then_inc(v_dma[s], 16)

            def load_raw(unit):
                r = unit % 3
                sp.dma_start(w_raw[:, r * WCOLS:(r + 1) * WCOLS], weights[unit, :, :]).then_inc(raw_dma, 16)

            def store_base(t, j, s):
                sp.wait_ge(base_ready, t + 1)
                sp.dma_start(base_dram[cols(t * P, P), :], x1[:, s, j, :]).then_inc(base_dma[s], 16)

            def batch(b, k, s, more):
                if more:
                    wait(sp, var2_ready, b)
                    load_x(b + 1, None, 1 - s)
                    wait(sp, v_used, b)
                    load_v(b + 1, None, 1 - s)
                if not isinstance(b, int) or b >= 2:
                    store_base(2 * b - 3, 1, s)
                if not isinstance(b, int) or b >= 1:
                    store_base(2 * b - 2, 0, 1 - s)
                sp.wait_ge(xn_ready, b + 1)
                sp.dma_start(xn_dram[cols(b * T, T), :].rearrange("(j p) c -> p j c", p=P),
                             xn[:, :, :]).then_inc(xn_dma, 16)

            load_x(0, 0, 0)
            sp.dma_start(wrow[0:1, :], w_row).then_inc(const_in, 16)
            sp.dma_start(wrow[32:33, :], w_row).then_inc(const_in, 16)
            sp.dma_start(w_ch[:, :], wu_ch[:, 0:CT]).then_inc(const_in, 16)
            sp.dma_start(u_ch[:, :], wu_ch[:, CT:2 * CT]).then_inc(const_in, 16)
            load_v(0, 0, 0)
            sp.dma_start(gate_f, gate_t.rearrange("p (a e) -> p a e", a=CT)).then_inc(const_in, 16)
            sp.dma_start(bias_sb[:, :], bias).then_inc(const_in, 16)
            load_raw(0)
            sp.wait_ge(raw_dma, 16)
            sp.sem_inc(raw_ready, 1)
            load_raw(1)
            sp.wait_ge(raw_dma, 32)
            sp.sem_inc(raw_ready, 1)
            batch(0, 0, 0, True)
            load_raw(2)
            batch(1, 0, 1, True)
            for unit in (3, 4):
                sp.wait_ge(split_lo, unit - 2)
                load_raw(unit)
            with sp.Fori(0, 2) as i:
                batch(2 * i + 2, i + 1, 0, True)
                batch(2 * i + 3, i + 1, 1, True)
            batch(6, 3, 0, True)
            batch(7, 3, 1, False)
            store_base(TILES - 3, 1, 0)
            store_base(TILES - 2, 0, 1)
            store_base(TILES - 1, 1, 1)
            sp.wait_ge(raw_dma, 16 * 5)
            sp.sem_inc(raw_ready, 3)
            sp.wait_ge(xn_dma, 16 * B)
            sp.wait_ge(steps_ready, 1)
            for unit in range(5, UNITS):
                until = sp.value_load(ends_i[0:1, unit - 5:unit - 4], min_val=1, max_val=STEPS + 1)
                sp.wait_ge(step_done, until)
                load_raw(unit)
                sp.wait_ge(raw_dma, 16 * (unit + 1))
                sp.sem_inc(raw_ready, 1)
            for s in range(2):
                sp.wait_ge(base_dma[s], 16 * TILES // 2)

            def load_res(t, s):
                sp.dma_start(res[s], base_dram[cols(t * P, P), :]).then_inc(res_dma[s], 16)

            load_res(0, 0)
            load_res(1, 1)
            with sp.Fori(0, TILES // 2 - 1) as i:
                for s in range(2):
                    sp.wait_ge(part_ready, 2 * i + s + 1)
                    load_res(2 * i + 2 + s, s)

        @block.gpsimd
        def _(pool):
            mk = Marks(pool, pool_mk)
            a = mk.mark(pool.memset(ident[:, :], 0.0))
            pool.memset(h_sb[:, :, :], 0.0)
            pool.memset(p_st[:, :, :], 0.0)
            pool.memset(q_st[:, :, :], 0.0)
            pool.memset(r_buf[:, :, :], 0.0)
            pool.memset(minus_half[:, :], -0.5)
            pool.iota(iota_i[:, :], pattern=[[1, T]], base=0, channel_multiplier=0)
            b = mk.mark(pool.iota(row_ii[:, :], pattern=[[0, 1]], base=0, channel_multiplier=1))
            mk.need(b)
            pool.affine_select(out=ident[:, :], in_=ident[:, :], compare_op=ALU.not_equal, fill=1.0,
                               base=0, pattern=[[-1, P]], channel_multiplier=1).then_inc(pool_const, 1)

            def rstd_of(n):
                var = moments[:, n, :, 1:2].rearrange("p j o -> p (j o)")
                pool.sem_inc(pool_passed, 1)
                d = mk.mark(pool.tensor_scalar(rstd[:, n, :], var, EPS, None, ALU.add))
                mk.need(d)
                return pool.tensor_tensor(rstd[:, n, :], rstd[:, n, :], minus_half[:, :], ALU.pow)

            def rstd1(b):
                wait(pool, var1_ready, b + 1)
                rstd_of(0).then_inc(rstd1_ready, 1)

            def rstd2(b):
                wait(pool, var2_ready, b + 1)
                rstd_of(1).then_inc(rstd2_ready, 1)

            rstd1(0)
            for half in range(HALVES):
                pool.wait_ge(split_hi, half + 1)
                pool.tensor_tensor(w_lo[:, half, :], w_raw[:, half * WCOLS:(half + 1) * WCOLS],
                                   w_hi[:, half, :].bitcast(F32), ALU.subtract).then_inc(split_lo, 1)
                if half == 0:
                    rstd1(1)
                    rstd2(0)
            mk.start(4)

            def batch(b, more):
                if more:
                    rstd1(b + 1)
                rstd2(b)

            mk.start(2 + 3)
            batch(1, True)
            assert mk.k == 2
            with pool.Fori(0, 2) as i:
                mk.start(7 + 4 * i)
                batch(2 * i + 2, True)
                batch(2 * i + 3, True)
                assert mk.k == 4
            mk.start(15)
            batch(6, True)
            batch(7, False)

            pool.wait_ge(idx_ready, 1)
            pool.wait_ge(xn_dma, 16 * B)

            def gather(s, k, par):
                if not isinstance(s, int) or s >= 2:
                    pool.wait_ge(xg_dma[par], 16 * k)
                pool.tensor_copy(idx_col[:, par:par + 1], idx_tab[:, cols(s, 1)]).then_inc(idx_set, 1)
                pool.wait_ge(idx_set, s + 1)
                wait(pool, b_xt_done, s - 1)
                pool.sem_inc(pool_passed, 1)
                pool.indirect_dma_start(xg[par], None, xn_dram[:, :],
                                        bass.IndirectOffsetOnAxis(ap=idx_col[:, par:par + 1].bitcast(U32), axis=0)
                                        ).then_inc(xg_dma[par], 16)

            gather(0, 0, 0)
            gather(1, 0, 1)
            with pool.Fori(1, STEPS // 2) as i:
                gather(2 * i, i, 0)
                gather(2 * i + 1, i, 1)
            gather(STEPS - 1, STEPS // 2, 0)

            pool.wait_ge(ys_ready, STEPS)
            pool.wait_ge(ys_dma[0], 16 * (STEPS // 2 + 1))
            pool.wait_ge(ys_dma[1], 16 * (STEPS // 2))

            def fetch(t, k, par):
                if not isinstance(t, int) or t >= 2:
                    for c in range(TOPK):
                        pool.wait_ge(yg_dma[par][c], 16 * k)
                pool.tensor_copy(y_idx[:, par, :], slot_i.rearrange("p t k -> p (t k)")[:, cols(2 * t, 2)]
                                 ).then_inc(yidx_set, 1)
                pool.wait_ge(yidx_set, t + 1)
                wait(pool, out_ready, t - 1)
                pool.sem_inc(pool_passed, 1)
                for c in range(TOPK):
                    pool.indirect_dma_start(yg[par][:, c, :], None, ys_dram[:, :],
                                            bass.IndirectOffsetOnAxis(ap=y_idx[:, par, c:c + 1].bitcast(U32), axis=0)
                                            ).then_inc(yg_dma[par][c], 16)

            fetch(0, 0, 0)
            fetch(1, 0, 1)
            with pool.Fori(1, TILES // 2) as i:
                fetch(2 * i, i, 0)
                fetch(2 * i + 1, i, 1)

        @block.scalar
        def _(act):
            for half in range(HALVES):
                act.wait_ge(raw_ready, half + 1)
                act.activation(w_hi[:, half, :], w_raw[:, half * WCOLS:(half + 1) * WCOLS], ACT.Copy
                               ).then_inc(split_hi, 1)

            def part_exp(b, k, s):
                wait(act, y_ready, b)
                for h in range(2):
                    wait(act, k_done, 2 * b + h + 1)
                    act.activation(e2[:, 2 * h:2 * h + 2, :].rearrange("p a t -> p (a t)"), ky[:, h, :], ACT.Exp
                                   ).then_inc(e2_ready, 1)
                for h in range(2):
                    wait(act, rarg_ready, 2 * b + h + 1)
                    act.activation(r_buf[:, 2 * h:2 * h + 2, :], r_buf[:, 2 * h:2 * h + 2, :], ACT.Exp
                                   ).then_inc(r_ready, 1)

            def unit(n, u):
                par = u % 2
                wait(act, g_done, n + 1)
                wait(act, h_ready, n - 1)
                act.activation(silu_g[:, par, :], g_ps[:, 0:H], ACT.Silu).then_inc(silu_ready, 1)
                wait(act, ht_done, n + 1)
                wait(act, down_done, n - 1)
                act.activation(h_hi[:, par, :, :].rearrange("p a t -> p (a t)"), ht_ps[:, 0:HC * P], ACT.Copy
                               ).then_inc(hhi_ready, 1)

            def part_x(b, k, s):
                for j in range(TJ):
                    wait(act, xt_done, 2 * b + j + 1)
                    wait(act, down_done, PER_BATCH * (b - 1))
                    act.activation(x_hi[:, s, j, :, :].rearrange("p a t -> p (a t)"), xt_ps[:, j, :], ACT.Copy
                                   ).then_inc(xhi_ready, 1)
                wait(act, logit_done, b + 1)
                act.activation(score.rearrange("p t e -> p (t e)")[:, cols(b * TJ * E, TJ * E)], logit_ps,
                               ACT.Exp, scale=-1.0).then_inc(score_ready, 1)

            def batch(b, k, s, units):
                part_exp(b, k, s)
                for u in range(units):
                    unit(PER_BATCH * (b - 1) + u, u)
                part_x(b, k, s)

            act.wait_ge(dve_const, 1)
            act.activation(decay[:, :], decay[:, :], ACT.Exp).then_inc(act_mk, 1)
            batch(0, 0, 0, 0)
            batch(1, 0, 1, PER_BATCH)
            with act.Fori(0, 2) as i:
                batch(2 * i + 2, i + 1, 0, PER_BATCH)
                batch(2 * i + 3, i + 1, 1, PER_BATCH)
            batch(6, 3, 0, PER_BATCH)
            batch(7, 3, 1, PER_BATCH)
            for u in range(PER_BATCH):
                unit(PER_BATCH * (B - 1) + u, u)

            def turned(s, par):
                wait(act, b_xt_done, s + 1)
                wait(act, b_u_done, s - 1)
                act.activation(xt[par], xt_ps[:, par, :], ACT.Copy).then_inc(b_xt_ready, 1)

            def gate(s, par):
                wait(act, b_g_done, s + 1)
                wait(act, b_h_ready, s - 1)
                act.activation(silu_g[:, par, :], g_ps[:, 0:H], ACT.Silu).then_inc(b_silu_ready, 1)

            def result(s, k, par):
                wait(act, step_done, s + 2)
                if not isinstance(s, int) or s >= 2:
                    act.wait_ge(ys_dma[par], 16 * k)
                act.activation(ys[par], d_ps[:, :], ACT.Copy).then_inc(ys_ready, 1)
                wait(act, ys_ready, s + 1)
                act.dma_start(ys_dram[cols(s * P, P), :], ys[par]).then_inc(ys_dma[par], 16)

            turned(0, 0)
            gate(0, 0)
            turned(1, 1)

            def pair(i):
                for par in (1, 0):
                    s = 2 * i + 2 - par
                    gate(s, par)
                    turned(s + 1, 1 - par)
                    result(s - 1, i, 1 - par)

            pair(0)
            with act.Fori(1, (STEPS - 3) // 2) as i:
                pair(i)
            gate(STEPS - 2, 1)
            turned(STEPS - 1, 0)
            result(STEPS - 3, (STEPS - 3) // 2, 0)
            gate(STEPS - 1, 0)
            result(STEPS - 2, (STEPS - 3) // 2, 1)
            result(STEPS - 1, (STEPS - 1) // 2, 0)

            def store(t, par):
                act.wait_ge(out_ready, t + 1)
                act.dma_start(out[cols(t * P, P), :], acc[par]).then_inc(out_dma[par], 16)

            with act.Fori(0, TILES // 2) as i:
                store(2 * i, 0)
                store(2 * i + 1, 1)
            for par in range(2):
                act.wait_ge(out_dma[par], 16 * TILES // 2)

        @block.vector
        def _(dve):
            mk = Marks(dve, dve_mk)
            dve.wait_ge(const_in, 16 * N_CONST)
            a = mk.mark(dve.tensor_scalar(u_first[:, :], w_ch[:, :], 0.0, None, ALU.max))
            dve.tensor_scalar(decay[:, :], w_ch[:, :], 0.0, None, ALU.min).then_inc(dve_const, 1)
            mk.need(a)
            mk.mark(dve.tensor_tensor(u_first[:, :], u_first[:, :], u_ch[:, :], ALU.add))
            c0 = mk.mark(dve.memset(neg_w[:, :].bitcast(F32), 0.0))
            dve.memset(ramp[:, :].bitcast(F32), 0.0)
            for row in (0, 32):
                c1 = mk.mark(dve.tensor_scalar(wrow[row:row + 1, :], wrow[row:row + 1, :], -1.0, 0.0,
                                               ALU.mult, ALU.min))
            mk.need(c1)
            for row in (0, 32):
                c2 = mk.mark(dve.tensor_copy(neg_w[row:row + 1, :], wrow[row:row + 1, :]))
            mk.need(c2)
            dve.tensor_tensor(neg_w[32:33, :], wrow[32:33, :], neg_w[32:33, :].bitcast(F32), ALU.subtract)
            dve.wait_ge(pool_const, 1)
            for row in (0, 32):
                dve.tensor_copy(ramp[row:row + 1, :], iota_i[row:row + 1, :])
            mk.mark(dve.tensor_copy(iota_f[:, :], iota_i[:, :]))
            d0 = mk.mark(dve.tensor_copy(gate_hi[:, :, :], gate_f[:, :, :]))
            mk.need(d0)
            d1 = mk.mark(dve.tensor_tensor(gate_lo[:, :, :], gate_f[:, :, :], gate_hi[:, :, :].bitcast(F32),
                                           ALU.subtract))
            mk.need(d1)
            dve.nop().then_inc(dve_const, 1)

            def moments_of(n, j, tile):
                m = mk.mark(dve.bn_stats(stats[:, n, j, :], tile))
                mk.need(m)
                dve.sem_inc(dve_passed, 1)
                return dve.bn_aggr(moments[:, n, j, :], stats[:, n, j, :])

            def key_moments(b, k, s):
                wait(dve, x_dma[s], 16 * (k + 1))
                mk.mark(moments_of(0, 0, x_in[:, s, 0, :]))
                moments_of(0, 1, x_in[:, s, 1, :]).then_inc(var1_ready, 1)

            def norm(dst, src, n):
                for j in range(TJ):
                    last = dve.tensor_scalar(dst(j), src(j), moments[:, n, j, 0:1], rstd[:, n, j:j + 1],
                                             ALU.subtract, ALU.mult)
                return last

            def keys(b, k, s):
                wait(dve, rstd1_ready, b + 1)
                wait(dve, k_done, 2 * b)
                norm(lambda j: k_tok[:, j, :], lambda j: x_in[:, s, j, :], 0).then_inc(ktok_ready, 1)

            def unit(n, u, base=True):
                par = u % 2
                wait(dve, u_done, n + 1)
                wait(dve, silu_ready, n + 1)
                wait(dve, ht_done, n - 1)
                dve.tensor_tensor(h_sb[:, par, 0:H], silu_g[:, par, :], u_ps[:, 0:H], ALU.mult
                                  ).then_inc(h_ready, 1)
                wait(dve, hhi_ready, n + 1)
                dve.tensor_tensor(h_lo[:, par, :, :].rearrange("p a t -> p (a t)"), ht_ps[:, 0:HC * P],
                                  h_hi[:, par, :, :].rearrange("p a t -> p (a t)").bitcast(F32), ALU.subtract
                                  ).then_inc(hlo_ready, 1)

            def add_base(n, j, s):
                wait(dve, down_done, n + 1)
                dve.tensor_tensor(x1[:, s, j, :], x1[:, s, j, :], d_ps[:, :], ALU.add).then_inc(base_ready, 1)

            def half(buf, h, lo=0, n=T):
                return buf[:, 2 * h:2 * h + 2, :]

            def batch(b, k, s, units, more):
                n0 = PER_BATCH * (b - 1)
                for h in range(2):
                    wait(dve, e2_ready, 2 * b + h + 1)
                    for c in (2 * h, 2 * h + 1):
                        last = dve.tensor_scalar(r_buf[:, c, 1:T], ky[:, h, (c % 2) * T + 1:(c % 2) * T + T],
                                                 u_first[:, c:c + 1], R_CAP, ALU.add, ALU.min)
                    last.then_inc(rarg_ready, 1)
                    if h == 0:
                        wait(dve, v_dma[s], 16 * (k + 1))
                    m_ev = mk.mark(dve.tensor_tensor(half(ev, h), half(e2, h), v_in[:, s, 2 * h:2 * h + 2, :],
                                                     ALU.mult))
                if units:
                    unit(n0, 0)
                    if not isinstance(b, int) or b >= 2:
                        add_base(n0 - 1, 1, s)
                mk.need(m_ev)
                for c in range(CT):
                    dve.tensor_tensor_scan(p_st[:, c, 1:T], decay[:, c:c + 1].broadcast_to([P, T - 1]),
                                           ev[:, c, 0:T - 1], 0.0, ALU.mult, ALU.add)
                    m_scan = mk.mark(dve.tensor_tensor_scan(
                        q_st[:, c, 1:T], decay[:, c:c + 1].broadcast_to([P, T - 1]),
                        e2[:, c, 0:T - 1], 0.0, ALU.mult, ALU.add))
                if units:
                    unit(n0 + 1, 1)
                wait(dve, r_ready, 2 * b + 2)
                mk.need(m_scan)
                m_rv = mk.mark(dve.tensor_tensor(ev[:, :, :], r_buf[:, :, :], v_in[:, s, :, :], ALU.mult))
                m_den = mk.mark(dve.tensor_tensor(e2[:, :, :], r_buf[:, :, :], q_st[:, :, :], ALU.add))
                if units:
                    unit(n0 + 2, 2)
                    add_base(n0 + 1, 0, 1 - s)
                mk.need(m_den)
                dve.memset(r_buf[:, :, 0:1], 0.0)
                m_num = mk.mark(dve.tensor_tensor(ev[:, :, :], ev[:, :, :], p_st[:, :, :], ALU.add))
                m_rec = mk.mark(dve.reciprocal(e2[:, :, :], e2[:, :, :]))
                mk.need(m_rec)
                m_y = dve.tensor_tensor(ev[:, :, :], ev[:, :, :], e2[:, :, :], ALU.mult)
                m_y.then_inc(y_ready, 1)
                dve.nop().then_inc(v_used, 1)
                if more:
                    key_moments(b + 1, k if s == 0 else k + 1, 1 - s)
                for j in range(TJ):
                    wait(dve, y_done, 2 * b + j + 1)
                    if j == 0:
                        if not isinstance(b, int) or b >= 2:
                            dve.wait_ge(base_dma[s], 32 * k)
                    m = mk.mark(dve.tensor_tensor(x1[:, s, j, :], x_in[:, s, j, :], ky[:, j, :], ALU.add))
                    mk.need(m)
                    last = moments_of(1, j, x1[:, s, j, :])
                    if j == 0:
                        mk.mark(last)
                last.then_inc(var2_ready, 1)
                if more:
                    keys(b + 1, None, 1 - s)
                if units:
                    unit(n0 + 3, 3)
                wait(dve, rstd2_ready, b + 1)
                wait(dve, xn_dma, 16 * b)
                wait(dve, xt_done, 2 * b)
                norm(lambda j: xn[:, j, :], lambda j: x1[:, s, j, :], 1).then_inc(xn_ready, 1)
                for j in range(TJ):
                    wait(dve, xhi_ready, 2 * b + j + 1)
                    dve.tensor_tensor(x_lo[:, s, j, :, :].rearrange("p a t -> p (a t)"), xt_ps[:, j, :],
                                      x_hi[:, s, j, :, :].rearrange("p a t -> p (a t)").bitcast(F32),
                                      ALU.subtract).then_inc(xlo_ready, 1)

            key_moments(0, 0, 0)
            keys(0, 0, 0)
            dve.wait_ge(act_mk, 1)
            batch(0, 0, 0, False, True)
            per0 = mk.k
            batch(1, 0, 1, True, True)
            start2, per = mk.k, mk.k - per0
            with dve.Fori(0, 2) as i:
                mk.start(start2 + 2 * per * i)
                batch(2 * i + 2, i + 1, 0, True, True)
                batch(2 * i + 3, i + 1, 1, True, True)
                assert mk.k == 2 * per
            mk.start(start2 + 4 * per)
            batch(6, 3, 0, True, True)
            batch(7, 3, 1, True, False)

            def bc(ap, dim, n):
                shape = list(ap.shape)
                shape.insert(dim, n)
                return ap.unsqueeze(dim).broadcast_to(shape)

            def chain(ins):
                mk.need(mk.mark(ins))

            def scores():
                dve.wait_ge(score_ready, B)
                chain(dve.tensor_scalar(score[:, :, :], score[:, :, :], 1.0, None, ALU.add))
                chain(dve.reciprocal(score[:, :, :], score[:, :, :]))
                chain(dve.tensor_tensor(biased[:, :, :], score[:, :, :], bc(bias_sb[:, :], 1, TILES), ALU.add))
                for t in range(TILES):
                    m = mk.mark(dve.max(top_v[:, t, :], biased[:, t, :]))
                mk.need(m)
                for t in range(TILES):
                    m = mk.mark(dve.max_index(top_i[:, t, :], top_v[:, t, :], biased[:, t, :]))
                mk.need(m)
                chain(dve.tensor_copy(top_f[:, :, :], top_i[:, :, 0:TOPK]))

            def choose():
                for k in range(TOPK):
                    m = mk.mark(dve.tensor_tensor(onehot[:, :, k, :], bc(iota_f[:, 0:E], 1, TILES),
                                                  bc(top_f[:, :, k], 2, E), ALU.is_equal))
                mk.need(m)
                chain(dve.tensor_tensor(chosen.rearrange("p e t -> p t e"), onehot[:, :, 0, :],
                                        onehot[:, :, 1, :], ALU.add))
                chain(dve.memset(first0[:, :, :], 1.0))
                chain(dve.memset(first0[:, :, 0:1], 0.0))
                flat = lambda ap: ap.rearrange("p e t -> p (e t)")
                dve.tensor_copy(chosen_b[:, :], flat(chosen[:, :, :]))
                chain(dve.tensor_tensor_scan(flat(upto[:, :, :]), flat(first0[:, :, :]), flat(chosen[:, :, :]),
                                             0.0, ALU.mult, ALU.add))
                dve.tensor_copy(total_b[:, :], upto[:, :, TILES - 1])
                dve.memset(ones_b[:, :], 1.0)
                dve.tensor_copy(row_id[:, :], row_ii[:, :])
                dve.memset(ones8[:, :], 1.0)
                chain(dve.tensor_tensor(before_b[:, :], flat(upto[:, :, :]), flat(chosen[:, :, :]), ALU.subtract))
                dve.tensor_scalar(tri[:, :], iota_f[:, 0:P], row_id[:, 0:1], None, ALU.is_gt
                                  ).then_inc(chosen_ready, 1)

            def gates():
                for k in range(TOPK):
                    m = mk.mark(dve.tensor_tensor(picked[:, :, k, :], onehot[:, :, k, :], score[:, :, :], ALU.mult))
                mk.need(m)
                chain(dve.reduce_sum(w_top[:, :, :], picked[:, :, :, :], AX.X))
                chain(dve.tensor_tensor(w_sum[:, :], w_top[:, :, 0], w_top[:, :, 1], ALU.add))
                chain(dve.reciprocal(w_sum[:, :], w_sum[:, :]))
                dve.tensor_tensor(w_tok[:, :, :], w_top[:, :, :], bc(w_sum[:, :], 2, TOPK), ALU.mult)
                dve.tensor_scalar(token_id[:, :], iota_f[:, 0:TILES], float(P), row_id[:, 0:1], ALU.mult, ALU.add)

            def places():
                dve.wait_ge(rank_done, 1)
                chain(dve.tensor_scalar(n_i[:, :], count_ps, float(P - 1), None, ALU.add))
                chain(dve.tensor_scalar(n_i[:, :], n_i[:, :], 7, None, ALU.logical_shift_right))
                chain(dve.tensor_copy(n_tiles[:, :], n_i[:, :]))
                chain(dve.tensor_tensor_scan(ends[:, :], ones8[:, :], n_tiles[:, :], 0.0, ALU.mult, ALU.add))
                chain(dve.tensor_tensor(starts[:, :], ends[:, :], n_tiles[:, :], ALU.subtract))
                chain(dve.scalar_tensor_tensor(place[:, :, :], bc(starts[:, :], 2, TILES), float(P),
                                               rank_ps.rearrange("p (e t) -> p e t", e=E), ALU.mult, ALU.add))
                for k in range(TOPK):
                    m = mk.mark(dve.tensor_tensor(picked[:, :, k, :], onehot[:, :, k, :],
                                                  place.rearrange("p e t -> p t e"), ALU.mult))
                mk.need(m)
                chain(dve.reduce_sum(slot_f[:, :, :], picked[:, :, :, :], AX.X))
                chain(dve.tensor_copy(slot_i[:, :, :], slot_f[:, :, :]))
                dve.tensor_scalar(part_i[:, 0, :, :], slot_i[:, :, :], P - 1, None, ALU.bitwise_and)
                chain(dve.tensor_scalar(part_i[:, 1, :, :], slot_i[:, :, :], 7, None, ALU.logical_shift_right))
                chain(dve.tensor_copy(part_f[:, :, :, :], part_i[:, :, :, :]))
                for t in range(TILES):
                    for k in range(TOPK):
                        n = t * TOPK + k
                        wait(dve, onehot_used, n - 1)
                        dve.tensor_scalar(at_row[:, k, :], iota_f[:, 0:P], part_f[:, 0, t, k:k + 1], None,
                                          ALU.is_equal)
                        dve.tensor_scalar(at_step[:, k, :], iota_f[:, 0:STEPS_PAD], part_f[:, 1, t, k:k + 1],
                                          token_id[:, t:t + 1], ALU.is_equal, ALU.mult
                                          ).then_inc(onehot_ready, 1)

            def steps():
                chain(dve.tensor_tensor(past[:, :, :], bc(iota_f[:, 0:STEPS_PAD], 1, E - 1),
                                        bc(ends[:, 0:E - 1], 2, STEPS_PAD), ALU.is_ge))
                chain(dve.reduce_sum(of_step[:, :], past.rearrange("p e s -> p s e"), AX.X))
                dve.tensor_scalar(w_need[:, :], of_step[:, :], float(HALVES + 1), None, ALU.add)
                chain(dve.tensor_scalar(w_off_f[:, :], of_step[:, :], float(HALVES), None, ALU.add))
                for e in range(0, E - 1, 3):
                    chain(dve.scalar_tensor_tensor(w_off_f[:, :], past[:, e, :], -3.0, w_off_f[:, :],
                                                   ALU.mult, ALU.add))
                dve.tensor_scalar(w_off[:, :], w_off_f[:, :], float(WCOLS), None, ALU.mult)
                chain(dve.tensor_scalar(ends_i[:, :], ends[:, :], 1.0, None, ALU.add))
                dve.nop().then_inc(steps_ready, 1)
                dve.wait_ge(onehot_used, TILES * TOPK)
                dve.tensor_copy(idx_tab[:, :], table_ps).then_inc(idx_ready, 1)

            n7 = PER_BATCH * (B - 1)
            unit(n7, 0)
            add_base(n7 - 1, 1, 0)
            scores()
            unit(n7 + 1, 1)
            choose()
            unit(n7 + 2, 2)
            add_base(n7 + 1, 0, 1)
            gates()
            unit(n7 + 3, 3)
            places()
            steps()
            add_base(n7 + 3, 1, 1)

            def hidden(s, par):
                wait(dve, b_u_done, s + 1)
                wait(dve, b_silu_ready, s + 1)
                wait(dve, b_turn_done, s - 1)
                dve.tensor_tensor(h_sb[:, par, 0:H], silu_g[:, par, :], u_ps[:, 0:H], ALU.mult
                                  ).then_inc(b_h_ready, 1)
                wait(dve, b_turn_done, s + 1)
                wait(dve, step_done, s)
                dve.tensor_copy(ht[par][:, 0:HC * P], ht_ps[:, 0:HC * P]).then_inc(b_ht_ready, 1)

            hidden(0, 0)
            hidden(1, 1)
            hidden(2, 0)
            with dve.Fori(1, STEPS // 2) as i:
                hidden(2 * i + 1, 1)
                hidden(2 * i + 2, 0)

            def combine(t, k, par):
                for c in range(TOPK):
                    wait(dve, yg_dma[par][c], 16 * (k + 1))
                wait(dve, res_dma[par], 16 * (k + 1))
                if not isinstance(t, int) or t >= 2:
                    dve.wait_ge(out_dma[par], 16 * k)
                w = w_tok.rearrange("p t k -> p (t k)")
                dve.scalar_tensor_tensor(acc[par], yg[par][:, 0, :], w[:, cols(2 * t, 1)], res[par],
                                         ALU.mult, ALU.add).then_inc(part_ready, 1)
                dve.wait_ge(part_ready, t + 1)
                dve.scalar_tensor_tensor(acc[par], yg[par][:, 1, :], w[:, cols(2 * t + 1, 1)], acc[par],
                                         ALU.mult, ALU.add).then_inc(out_ready, 1)

            combine(0, 0, 0)
            combine(1, 0, 1)
            with dve.Fori(1, TILES // 2) as i:
                combine(2 * i, i, 0)
                combine(2 * i + 1, i, 1)

        @block.tensor
        def _(pe):
            def keys(b, k, s):
                wait(pe, ktok_ready, b + 1)
                wait(pe, var2_ready, b)
                for h in range(2):
                    for c in (2 * h, 2 * h + 1):
                        region = ky[:, h, (c % 2) * T:(c % 2) * T + T]
                        pe.matmul(region, neg_w[:, c * P:(c + 1) * P], ramp[:, :], start=True, stop=False)
                        for j in range(TJ):
                            last = pe.matmul(region[:, j * P:(j + 1) * P], k_tok[:, j, c * P:(c + 1) * P],
                                             ident[:, :], start=False, stop=(j == TJ - 1))
                    last.then_inc(k_done, 1)

            def y_turn(b):
                wait(pe, y_ready, b + 1)
                for j in range(TJ):
                    for c in range(CT):
                        last = pe.transpose(ky[:, j, c * P:(c + 1) * P], ev[:, c, j * P:(j + 1) * P], ident[:, :])
                    last.then_inc(y_done, 1)

            def x_turn(b):
                wait(pe, xn_ready, b + 1)
                wait(pe, xlo_ready, 2 * b)
                for j in range(TJ):
                    for c in range(CT):
                        last = pe.transpose(xt_ps[:, j, c * P:(c + 1) * P], xn[:, j, c * P:(c + 1) * P],
                                            ident[:, :])
                    last.then_inc(xt_done, 1)

            def product(dst, pairs, first=True, final=True):
                n = len(pairs)
                for i, (a_hi, a_lo, b_hi, b_lo) in enumerate(pairs):
                    pe.matmul(dst, a_hi, b_hi, start=(first and i == 0), stop=False)
                    pe.matmul(dst, a_hi, b_lo, start=False, stop=False)
                    last = pe.matmul(dst, a_lo, b_hi, start=False, stop=(final and i == n - 1))
                return last

            def logits(b, s):
                wait(pe, xlo_ready, 2 * b + 2)
                wait(pe, hlo_ready, PER_BATCH * b)
                for j in range(TJ):
                    last = product(logit_ps[:, j * E:(j + 1) * E],
                                   [(x_hi[:, s, j, c, :], x_lo[:, s, j, c, :], gate_hi[:, c, :], gate_lo[:, c, :])
                                    for c in range(CT)])
                last.then_inc(logit_done, 1)

            def unit(n, u, s, logit_batches=None, first=False):
                j, half, par = u // HALVES, u % HALVES, u % 2
                if u == 0:
                    wait(pe, xlo_ready, (n + PER_BATCH) // 2 if isinstance(n, int) else logit_batches * 2)
                wait(pe, silu_ready, n)
                for bank, off, free, done in ((g_ps, 0, None, g_done), (u_ps, H, h_ready, u_done)):
                    if free is not None:
                        wait(pe, free, n)
                    product(bank[:, 0:H],
                            [(x_hi[:, s, j, c, :], x_lo[:, s, j, c, :],
                              w_hi[:, half, c * UP + off:c * UP + off + H],
                              w_lo[:, half, c * UP + off:c * UP + off + H]) for c in range(CT)]
                            ).then_inc(done, 1)
                if not first:
                    down(n - 1, (u - 1) % HALVES)
                if u == 0 and logit_batches is not None:
                    wait(pe, score_ready, logit_batches)
                wait(pe, h_ready, n + 1)
                for c in range(HC):
                    last = pe.transpose(ht_ps[:, c * P:(c + 1) * P], h_sb[:, par, c * P:(c + 1) * P], ident[:, :])
                last.then_inc(ht_done, 1)

            def down(n, half):
                wait(pe, hlo_ready, n + 1)
                if half == 0:
                    tile = (n // 2) if isinstance(n, int) else None
                    wait(pe, base_ready, tile if tile is not None else down_tile[0])
                product(d_ps[:, :],
                        [(h_hi[:, half, c, :], h_lo[:, half, c, :],
                          w_hi[:, half, DOWN0 + c * C:DOWN0 + (c + 1) * C],
                          w_lo[:, half, DOWN0 + c * C:DOWN0 + (c + 1) * C]) for c in range(HC)],
                        first=(half == 0), final=(half == 1)).then_inc(down_done, 1)

            down_tile = [None]

            def batch(b, s, units, more):
                n0 = PER_BATCH * (b - 1)
                for u in range(units):
                    if u == 3:
                        y_turn(b)
                    down_tile[0] = 2 * (b - 1) + (u - 1) // 2
                    unit(n0 + u, u, 1 - s, b, first=(isinstance(b, int) and b == 1 and u == 0))
                if not units:
                    y_turn(b)
                x_turn(b)
                if more:
                    keys(b + 1, None, None)
                logits(b, s)

            pe.wait_ge(pool_const, 1)
            pe.wait_ge(dve_const, 2)
            keys(0, 0, 0)
            batch(0, 0, 0, True)
            pe.wait_ge(split_lo, 2)
            batch(1, 1, PER_BATCH, True)
            with pe.Fori(0, 2) as i:
                batch(2 * i + 2, 0, PER_BATCH, True)
                batch(2 * i + 3, 1, PER_BATCH, True)
            batch(6, 0, PER_BATCH, True)
            batch(7, 1, PER_BATCH, False)

            n7 = PER_BATCH * (B - 1)
            for u in range(PER_BATCH):
                down_tile[0] = 2 * (B - 1) + (u - 1) // 2
                unit(n7 + u, u, 1, B)
                if u == 1:
                    pe.wait_ge(chosen_ready, 1)
                    pe.matmul(rank_ps, tri[:, :], chosen_b[:, :], start=True, stop=False)
                    pe.matmul(rank_ps, ones_b[:, :], before_b[:, :], start=False, stop=True)
                    pe.matmul(count_ps, ones_b[:, :], total_b[:, :], start=True, stop=True
                              ).then_inc(rank_done, 1)
            down(n7 + PER_BATCH - 1, 1)
            for n in range(TILES * TOPK):
                pe.wait_ge(onehot_ready, n + 1)
                pe.matmul(table_ps, at_row[:, n % 2, :], at_step[:, n % 2, :], start=(n == 0),
                          stop=(n == TILES * TOPK - 1)).then_inc(onehot_used, 1)

            def turn_x(s, k, par):
                wait(pe, xg_dma[par], 16 * (k + 1))
                wait(pe, b_xt_ready, s - 1)
                for c in range(CT):
                    last = pe.transpose(xt_ps[:, par, c * P:(c + 1) * P], xg[par][:, c * P:(c + 1) * P],
                                        ident[:, :])
                last.then_inc(b_xt_done, 1)

            def up(s, par):
                need = pe.value_load(w_need[0:1, cols(s, 1)], min_val=1, max_val=UNITS)
                off = pe.value_load(w_off[0:1, cols(s, 1)], min_val=0, max_val=2 * WCOLS)
                pe.wait_ge(raw_ready, need)
                wait(pe, b_xt_ready, s + 1)
                wait(pe, b_silu_ready, s)
                for bank, o, free, done in ((g_ps, 0, None, b_g_done), (u_ps, H, b_h_ready, b_u_done)):
                    if free is not None:
                        wait(pe, free, s)
                    for c in range(CT):
                        last = pe.matmul(bank[:, 0:H], xt[par][:, c * P:(c + 1) * P],
                                         w_raw[:, bass.DynSlice(off + (c * UP + o), H)],
                                         start=(c == 0), stop=(c == CT - 1))
                    last.then_inc(done, 1)

            def down_step(s, par):
                off = pe.value_load(w_off[0:1, cols(s, 1)], min_val=0, max_val=2 * WCOLS)
                wait(pe, b_ht_ready, s + 1)
                wait(pe, ys_ready, s)
                for c in range(HC):
                    last = pe.matmul(d_ps[:, :], ht[par][:, c * P:(c + 1) * P],
                                     w_raw[:, bass.DynSlice(off + (DOWN0 + c * C), C)],
                                     start=(c == 0), stop=(c == HC - 1))
                last.then_inc(step_done, 1)

            def turn_h(s, par):
                wait(pe, b_h_ready, s + 1)
                wait(pe, b_ht_ready, s)
                for c in range(HC):
                    last = pe.transpose(ht_ps[:, c * P:(c + 1) * P], h_sb[:, par, c * P:(c + 1) * P], ident[:, :])
                last.then_inc(b_turn_done, 1)

            pe.wait_ge(steps_ready, 1)
            pe.wait_ge(idx_ready, 1)
            pe.wait_ge(base_ready, TILES)
            pe.nop().then_inc(step_done, 1)
            turn_x(0, 0, 0)
            up(0, 0)
            turn_x(1, 0, 1)
            turn_h(0, 0)

            def pair(i):
                for par in (1, 0):
                    s = 2 * i + 2 - par
                    up(s, par)
                    turn_x(s + 1, i + 1, 1 - par)
                    down_step(s - 1, 1 - par)
                    turn_h(s, par)

            pair(0)
            with pe.Fori(1, (STEPS - 3) // 2) as i:
                pair(i)
            up(STEPS - 2, 1)
            turn_x(STEPS - 1, (STEPS - 1) // 2, 0)
            down_step(STEPS - 3, 0)
            turn_h(STEPS - 2, 1)
            up(STEPS - 1, 0)
            down_step(STEPS - 2, 1)
            turn_h(STEPS - 1, 0)
            down_step(STEPS - 1, 0)


def kernel(**inputs):
    import numpy as np
    from concourse import bacc
    from concourse import mybir as mb
    from concourse.bass_utils import run_bass_kernel_spmd as run

    a = {k: np.asarray(v) for k, v in inputs.items()}
    hs = HALVES * H

    def unit(up, down):
        w = np.zeros((P, WCOLS), np.float32)
        w[:, :DOWN0] = up.T.reshape(CT, P, UP).transpose(1, 0, 2).reshape(P, DOWN0)
        d = np.zeros((HC * P, C), np.float32)
        d[:H] = down.T
        w[:, DOWN0:] = d.reshape(HC, P, C).transpose(1, 0, 2).reshape(P, HC * C)
        return w

    sg, sd = a["L0_ffn_shared_gw"], a["L0_ffn_shared_dw"]
    units = [unit(np.concatenate([sg[hs + h * H:hs + (h + 1) * H], sg[h * H:(h + 1) * H]]),
                  sd[:, h * H:(h + 1) * H]) for h in range(HALVES)]
    units += [unit(a["L0_ffn_up_w"][e], a["L0_ffn_down_w"][e]) for e in range(E)]
    arrays = {
        "x_in_dram": np.ascontiguousarray(a["x"]).reshape(B * T, C),
        "ctx_t_dram": np.ascontiguousarray(a["ctx_2048"].transpose(0, 2, 1)).reshape(B * C, T),
        "w_row_dram": np.ascontiguousarray(a["L0_xattn_w"]).reshape(1, C),
        "wu_ch_dram": np.concatenate([a[n].reshape(CT, P).T for n in ("L0_xattn_w", "L0_xattn_u")], axis=1),
        "gate_t_dram": np.ascontiguousarray(a["L0_ffn_gate_w"].T.reshape(CT, P, E).transpose(1, 0, 2).reshape(P, CT * E)),
        "bias_dram": np.ascontiguousarray(np.broadcast_to(a["L0_ffn_gate_bias"], (P, E))),
        "weights_dram": np.stack(units),
    }
    nc = bacc.Bacc("TRN2", target_bir_lowering=False, num_devices=1)
    args = [nc.dram_tensor(n, v.shape, mb.dt.float32, kind="ExternalInput").ap() for n, v in arrays.items()]
    args.append(nc.dram_tensor("xn_scratch", (B * T, C), mb.dt.float32).ap())
    args.append(nc.dram_tensor("base_scratch", (B * T, C), mb.dt.float32).ap())
    args.append(nc.dram_tensor("ys_scratch", (STEPS * P, C), mb.dt.float32).ap())
    args.append(nc.dram_tensor("out_dram", (B * T, C), mb.dt.float32, kind="ExternalOutput").ap())
    build(nc, *args)
    r = run(nc, [arrays], core_ids=[0])
    return r.results[0]["out_dram"].reshape(B, T, C)
```

```python
import concourse.bass as bass
from concourse import mybir
from contextlib import ExitStack

F32 = mybir.dt.float32
F32R = mybir.dt.float32r
BF16 = mybir.dt.bfloat16
FP16 = mybir.dt.float16
I32 = mybir.dt.int32
U32 = mybir.dt.uint32
ALU = mybir.AluOpType
ACT = mybir.ActivationFunctionType
AX = mybir.AxisListType

P = 128
B, T, C = 8, 256, 512
CT = C // P
TJ = T // P
TILES = B * TJ
E, TOPK = 8, 2
H = 352
HALVES = 2
HC = 3
UP = 2 * H
WCOLS = CT * UP + HC * C
DOWN0 = CT * UP
UP0 = UP + E
WCOLS0 = CT * UP0 + HC * C
REGION_AT = [0, WCOLS0, WCOLS0 + WCOLS]
STEPS = TILES * TOPK + E - 1
STEPS_PAD = STEPS + 1
UNITS = HALVES + E
REGIONS = 3
PIECES = 4
PIECE = WCOLS // PIECES
PIECE0 = WCOLS0 // PIECES
SPARE_ROWS = P
PER_BATCH = TJ * HALVES
EPS = 1e-5


class Marks:

    def __init__(self, eng, sem):
        self.eng, self.sem, self.base, self.k = eng, sem, 0, 0

    def start(self, base):
        self.base, self.k = base, 0

    def mark(self, ins):
        self.k += 1
        ins.then_inc(self.sem, 1)
        return self.base + self.k

    def need(self, mark):
        self.eng.wait_ge(self.sem, mark)


def wait(eng, sem, value):
    if isinstance(value, int) and value <= 0:
        return
    eng.wait_ge(sem, value)


def piece_at(region, p, n=PIECE):
    return slice(REGION_AT[region] + p * n, REGION_AT[region] + (p + 1) * n)


def cols(start, n):
    return slice(start, start + n) if isinstance(start, int) else bass.DynSlice(start, n)


def build(nc, x, ctx_t, w_row, wu_ch, bias, weights, xn_dram, hi_dram, lo_dram, out):
    with ExitStack() as ctx:
        def sb(name, shape, dt=F32):
            return ctx.enter_context(nc.sbuf_tensor(name, shape, dt))

        def pb(name, shape, dt=F32):
            return ctx.enter_context(nc.psum_tensor(name, shape, dt))

        def sem(name):
            return ctx.enter_context(nc.semaphore(name))

        w_hi = sb("w_hi", [P, WCOLS0 + 2 * WCOLS], F32R)
        w_lo = sb("w_lo", [P, WCOLS0 + 2 * WCOLS], F32R)
        w_raw = sb("w_raw", [P, PIECES, PIECE0])
        ident = sb("ident", [P, P])
        ramp = sb("ramp", [P, T], F32R)
        neg_w = sb("neg_w", [P, C], F32R)
        iota_f = sb("iota_f", [P, T])
        row_id = sb("row_id", [P, 1])
        row_id1 = sb("row_id1", [P, 1])
        row_ii = sb("row_ii", [P, 1], I32)
        token_id = sb("token_id", [P, TILES])
        w_ch = sb("w_ch", [P, CT])
        u_ch = sb("u_ch", [P, CT])
        decay = sb("decay", [P, CT])
        state_log = sb("state_log", [P, CT])
        own_log = sb("own_log", [P, CT])
        lift = sb("lift", [P, CT])
        bias_sb = sb("bias_sb", [P, E])
        ones_b = sb("ones_b", [P, P], BF16)
        minus_half = sb("minus_half", [P, TJ])
        x_in = sb("x_in", [P, 2, TJ, C])
        v_in = sb("v_in", [P, 2, CT, T])
        k_tok = sb("k_tok", [P, TJ, C])
        stats = sb("stats", [P, 2, TJ, 6])
        moments = sb("moments", [P, 2, TJ, 2])
        rstd = sb("rstd", [P, 2, TJ])
        own = sb("own", [P, CT, T])
        e2 = sb("e2", [P, CT, T])
        ev = sb("ev", [P, CT, T])
        p_st = sb("p_st", [P, CT, T])
        q_st = sb("q_st", [P, CT, T])
        x1 = sb("x1", [P, 2, TJ, C])
        xn = sb("xn", [P, TJ, C])
        x_hi = sb("x_hi", [P, 2, TJ, CT, P], F32R)
        x_lo = sb("x_lo", [P, 2, TJ, CT, P], F32R)
        silu_g = sb("silu_g", [P, 2, H])
        h_sb = sb("h_sb", [P, 2, HC * P])
        h_hi = sb("h_hi", [P, 2, HC, P], F32R)
        h_lo = sb("h_lo", [P, 2, HC, P], F32R)
        score = sb("score", [P, TILES, E])
        top_f = sb("top_f", [P, TILES, TOPK])
        w_top = sb("w_top", [P, TILES, TOPK])
        w_tok = sb("w_tok", [P, TILES, TOPK])
        chosen_b = sb("chosen_b", [P, E * TILES], BF16)
        total_b = sb("total_b", [P, E], BF16)
        n_i = sb("n_i", [P, E], I32)
        n_tiles = sb("n_tiles", [P, E])
        ends = sb("ends", [P, E])
        starts = sb("starts", [P, E])
        ones8 = sb("ones8", [P, E])
        slot_f = sb("slot_f", [P, TILES, TOPK])
        slot_i = sb("slot_i", [P, TILES, TOPK], I32)
        part_i = sb("part_i", [P, 2, TILES, TOPK], I32)
        part_f = sb("part_f", [P, 2, TILES, TOPK])
        ends_i = sb("ends_i", [P, E], I32)
        spare_p = p_st.rearrange("p a t -> p (a t)")
        spare_q = q_st.rearrange("p a t -> p (a t)")
        onehot = spare_p[:, 0:256].rearrange("p (t k e) -> p t k e", t=TILES, k=TOPK)
        picked = spare_p[:, 256:512].rearrange("p (t k e) -> p t k e", t=TILES, k=TOPK)
        past = spare_p[:, 512:512 + (E - 1) * STEPS_PAD].rearrange("p (e s) -> p e s", e=E - 1)
        biased = spare_q[:, 0:128].rearrange("p (t e) -> p t e", t=TILES)
        top_v = spare_q[:, 128:256].rearrange("p (t e) -> p t e", t=TILES)
        chosen = spare_q[:, 256:384].rearrange("p (e t) -> p e t", e=E)
        upto = spare_q[:, 384:512].rearrange("p (e t) -> p e t", e=E)
        place = spare_q[:, 512:640].rearrange("p (e t) -> p e t", e=E)
        first0 = spare_q[:, 640:768].rearrange("p (e t) -> p e t", e=E)
        of_step = spare_p[:, 792:792 + STEPS_PAD]
        w_off_f = spare_p[:, 832:832 + STEPS_PAD]
        spare_v = v_in.rearrange("p s a t -> p (s a t)")
        at_row = spare_v[:, 0:4 * P].rearrange("p (k r) -> p k r", k=4)
        at_step = spare_v[:, 4 * P:4 * P + 8 * STEPS_PAD].rearrange("p (k a s) -> p k a s", k=4, a=2)
        slot_v = spare_v[:, 1024:1024 + STEPS_PAD]
        slot_no = spare_v[:, 1088:1088 + STEPS_PAD]
        dump = spare_v[:, 1152:1153]
        top_i = spare_v[:, 1160:1160 + TILES * 8].bitcast(U32).rearrange("p (t k) -> p t k", t=TILES)
        before_b = spare_v[:, 1296:1296 + E * TILES // 2].bitcast(BF16)
        w_sum = spare_v[:, 1392:1392 + TILES]
        step_ints = e2.rearrange("p a t -> p (a t)").bitcast(I32)
        w_off = step_ints[:, 0:STEPS_PAD]
        w_need = step_ints[:, 64:64 + STEPS_PAD]
        idx_tab = step_ints[:, 128:128 + 2 * STEPS_PAD].rearrange("p (a s) -> p a s", a=2)
        w_slot = own.rearrange("p a t -> p (a t)")[:, 0:STEPS_PAD]
        tri = spare_q[:, 936:1000].bitcast(BF16)
        wrow = x1[:, 1, 0, :]
        iota_i = x1[:, 1, 1, 0:T].bitcast(I32)
        gather_col = sb("gather_col", [P, 2], I32)
        add_col = sb("add_col", [P, 2], I32)
        xg = [k_tok[:, j, :] for j in range(2)]
        ys = [ev[:, 2 * j:2 * j + 2, :].rearrange("p a t -> p (a t)") for j in range(2)]

        ky = pb("ky", [P, 2, C])
        xt_ps = pb("xt_ps", [P, 2, C])
        g_ps = pb("g_ps", [P, C])
        u_ps = pb("u_ps", [P, C])
        ht_ps = pb("ht_ps", [P, C])
        d_ps = pb("d_ps", [P, C])
        logit_ps = ht_ps[:, HC * P:HC * P + TJ * E]
        rank_ps = xt_ps[:, 0, 0:E * TILES]
        count_ps = xt_ps[:, 0, E * TILES:E * TILES + E]
        table_ps = xt_ps[:, 1, 0:2 * STEPS_PAD]

        const_in = sem("const_in")
        pool_mk = sem("pool_mk")
        dve_mk = sem("dve_mk")
        dve_passed = sem("dve_passed")
        pool_passed = sem("pool_passed")
        sp_passed = sem("sp_passed")
        act_mk = sem("act_mk")
        x_dma = [sem(f"x_dma{s}") for s in range(2)]
        v_dma = [sem(f"v_dma{s}") for s in range(2)]
        xn_dma = sem("xn_dma")
        base_dma = [sem(f"base_dma{s}") for s in range(2)]
        raw_dma = [sem(f"raw_dma{p}") for p in range(PIECES)]
        split_dma = [sem(f"split_dma{p}") for p in range(PIECES)]
        zero_dma = sem("zero_dma")
        region_dma = [sem(f"region_dma{p}") for p in range(2)]
        w_ready = sem("w_ready")
        pool_const = sem("pool_const")
        zeros_ready = sem("zeros_ready")
        dve_const = sem("dve_const")
        split_hi = sem("split_hi")
        split_lo = sem("split_lo")
        var1_ready = sem("var1_ready")
        ktok_ready = sem("ktok_ready")
        k_done = sem("k_done")
        rstd1_ready = sem("rstd1_ready")
        rstd2_ready = sem("rstd2_ready")
        e2_ready = sem("e2_ready")
        own_ready = sem("own_ready")
        ev_ready = sem("ev_ready")
        x1_ready = sem("x1_ready")
        own_used = sem("own_used")
        p_ready = sem("p_ready")
        num_ready = sem("num_ready")
        y_ready = sem("y_ready")
        y_done = sem("y_done")
        var2_ready = sem("var2_ready")
        xn_ready = sem("xn_ready")
        xt_done = sem("xt_done")
        xhi_ready = sem("xhi_ready")
        xlo_ready = sem("xlo_ready")
        logit_done = sem("logit_done")
        score_ready = sem("score_ready")
        g_done = sem("g_done")
        u_done = sem("u_done")
        silu_ready = sem("silu_ready")
        h_ready = sem("h_ready")
        ht_done = sem("ht_done")
        hhi_ready = sem("hhi_ready")
        hlo_ready = sem("hlo_ready")
        down_done = sem("down_done")
        base_ready = sem("base_ready")
        chosen_ready = sem("chosen_ready")
        rank_done = sem("rank_done")
        onehot_ready = sem("onehot_ready")
        onehot_used = sem("onehot_used")
        steps_ready = sem("steps_ready")
        idx_ready = sem("idx_ready")
        idx_set = sem("idx_set")
        xg_dma = [sem(f"xg_dma{s}") for s in range(2)]
        b_xt_done = sem("b_xt_done")
        b_xhi_ready = sem("b_xhi_ready")
        b_xlo_ready = sem("b_xlo_ready")
        b_g_done = sem("b_g_done")
        b_u_done = sem("b_u_done")
        b_silu_ready = sem("b_silu_ready")
        b_h_ready = sem("b_h_ready")
        b_turn_done = sem("b_turn_done")
        b_hhi_ready = sem("b_hhi_ready")
        b_hlo_ready = sem("b_hlo_ready")
        step_done = sem("step_done")
        ys_ready = sem("ys_ready")
        add_set = sem("add_set")
        add_dma = sem("add_dma")

        N_CONST = 5
        block = ctx.enter_context(nc.Block())

        @block.sync
        def _(sp):
            def load_x(b, s):
                sp.dma_start(x_in[:, s, :, :],
                             x[cols(b * T, T), :].rearrange("(j p) c -> p j c", p=P)).then_inc(x_dma[s], 16)

            def load_v(b, s):
                sp.dma_start(v_in[:, s, :, :],
                             ctx_t[cols(b * C, C), :].rearrange("(a p) t -> p a t", p=P)).then_inc(v_dma[s], 16)

            def load_piece(unit, p):
                wait(sp, split_lo, PIECES * (unit - 1) + p + 1)
                n = PIECE0 if isinstance(unit, int) and unit == 0 else PIECE
                sp.dma_start(w_raw[:, p, 0:n], weights[cols(unit * P, P), p * n:(p + 1) * n]
                             ).then_inc(raw_dma[p], 16)

            def store_base(t, j, s):
                sp.wait_ge(base_ready, t + 1)
                sp.dma_start(out[cols(t * P, P), :], x1[:, s, j, :]).then_inc(base_dma[s], 16)

            def store_piece(b, p):
                at = piece_at(2, p)
                sp.wait_ge(split_lo, PIECES * (HALVES + b) + p + 1)
                sp.sem_inc(sp_passed, 1)
                sp.dma_start(hi_dram[cols((E - 1 - b) * P, P), p * PIECE:(p + 1) * PIECE], w_hi[:, at].bitcast(F32)
                             ).then_inc(split_dma[p], 16)
                sp.dma_start(lo_dram[cols((E - 1 - b) * P, P), p * PIECE:(p + 1) * PIECE], w_lo[:, at].bitcast(F32)
                             ).then_inc(split_dma[p], 16)

            def batch(b, s, more):
                if more:
                    wait(sp, var2_ready, b)
                    load_x(b + 1, 1 - s)
                    wait(sp, num_ready, b)
                    load_v(b + 1, 1 - s)
                if not isinstance(b, int) or b >= 2:
                    store_base(2 * b - 3, 1, s)
                for p in range(PIECES):
                    if not isinstance(b, int) or b >= 1:
                        store_piece(b - 1, p)
                    load_piece(HALVES + b, p)
                if not isinstance(b, int) or b >= 1:
                    store_base(2 * b - 2, 0, 1 - s)
                sp.wait_ge(xn_ready, b + 1)
                sp.dma_start(xn_dram[cols(b * T, T), :].rearrange("(j p) c -> p j c", p=P),
                             xn[:, :, :]).then_inc(xn_dma, 16)

            load_x(0, 0)
            sp.dma_start(wrow[0:1, :], w_row).then_inc(const_in, 16)
            sp.dma_start(wrow[32:33, :], w_row).then_inc(const_in, 16)
            sp.dma_start(w_ch[:, :], wu_ch[:, 0:CT]).then_inc(const_in, 16)
            sp.dma_start(u_ch[:, :], wu_ch[:, CT:2 * CT]).then_inc(const_in, 16)
            sp.dma_start(bias_sb[:, :], bias).then_inc(const_in, 16)
            load_v(0, 0)
            for p in range(PIECES):
                load_piece(0, p)
            load_x(1, 1)
            load_v(1, 1)
            sp.wait_ge(zeros_ready, 1)
            sp.dma_start(out[B * T:B * T + SPARE_ROWS, :], q_st[:, 0:2, :].rearrange("p a t -> p (a t)")
                         ).then_inc(zero_dma, 16)
            for p in range(PIECES):
                load_piece(1, p)
            batch(0, 0, False)
            batch(1, 1, True)
            with sp.Fori(0, 2) as i:
                batch(2 * i + 2, 0, True)
                batch(2 * i + 3, 1, True)
            batch(6, 0, True)
            batch(7, 1, False)
            store_base(TILES - 3, 1, 0)
            store_base(TILES - 2, 0, 1)

            sp.wait_ge(split_lo, PIECES * UNITS)
            sp.sem_inc(w_ready, 1)
            for p in range(PIECES):
                sp.wait_ge(split_dma[p], 32 * (E - 1))

            def load_expert(e):
                r = (e + 2) % REGIONS
                for p in range(PIECES):
                    at = piece_at(r, p)
                    rows, part = slice(e * P, (e + 1) * P), slice(p * PIECE, (p + 1) * PIECE)
                    sp.dma_start(w_hi[:, at].bitcast(F32), hi_dram[rows, part]).then_inc(region_dma[p % 2], 16)
                    sp.dma_start(w_lo[:, at].bitcast(F32), lo_dram[rows, part]).then_inc(region_dma[p % 2], 16)
                    if p > 0:
                        sp.wait_ge(region_dma[(p - 1) % 2], 32 * (PIECES // 2 * (e - 1) + (p - 1) // 2 + 1))
                sp.wait_ge(region_dma[1], 32 * PIECES // 2 * e)
                sp.sem_inc(w_ready, 1)

            sp.wait_ge(down_done, TILES * HALVES - 1)
            load_expert(1)
            store_base(TILES - 1, 1, 1)
            sp.wait_ge(down_done, TILES * HALVES)
            load_expert(2)
            sp.wait_ge(steps_ready, 1)
            for e in range(3, E):
                until = sp.value_load(ends_i[0:1, e - 3:e - 2], min_val=1, max_val=STEPS + 1)
                sp.wait_ge(step_done, until)
                load_expert(e)

        @block.gpsimd
        def _(pool):
            mk = Marks(pool, pool_mk)
            pool.memset(ident[:, :], 0.0)
            pool.memset(neg_w[:, :].bitcast(F32), 0.0)
            pool.memset(ramp[:, :].bitcast(F32), 0.0)
            pool.iota(row_ii[:, :], pattern=[[0, 1]], base=0, channel_multiplier=1)
            mk.need(mk.mark(pool.iota(iota_i[:, :], pattern=[[1, T]], base=0, channel_multiplier=0)))
            pool.affine_select(out=ident[:, :], in_=ident[:, :], compare_op=ALU.not_equal, fill=1.0,
                               base=0, pattern=[[-1, P]], channel_multiplier=1).then_inc(pool_const, 1)
            pool.memset(minus_half[:, :], -0.5)
            pool.memset(h_sb[:, :, :], 0.0)
            mk.need(mk.mark(pool.memset(q_st[:, :, :], 0.0)))
            pool.sem_inc(zeros_ready, 1)

            def rstd_of(n):
                var = moments[:, n, :, 1:2].rearrange("p j o -> p (j o)")
                pool.sem_inc(pool_passed, 1)
                d = mk.mark(pool.tensor_scalar(rstd[:, n, :], var, EPS, None, ALU.add))
                mk.need(d)
                return pool.tensor_tensor(rstd[:, n, :], rstd[:, n, :], minus_half[:, :], ALU.pow)

            def rstd1(b):
                wait(pool, var1_ready, b + 1)
                rstd_of(0).then_inc(rstd1_ready, 1)

            def rstd2(b):
                wait(pool, var2_ready, b + 1)
                rstd_of(1).then_inc(rstd2_ready, 1)

            def numerator(b, s):
                wait(pool, own_ready, b + 1)
                wait(pool, ev_ready, b + 1)
                pool.sem_inc(pool_passed, 1)
                m = mk.mark(pool.tensor_tensor(v_in[:, s, :, :], v_in[:, s, :, :], own[:, :, :], ALU.mult))
                mk.need(m)
                pool.sem_inc(own_used, 1)
                wait(pool, p_ready, b + 1)
                pool.sem_inc(pool_passed, 1)
                pool.tensor_tensor(ev[:, :, :], p_st[:, :, :], v_in[:, s, :, :], ALU.add).then_inc(num_ready, 1)

            def split(unit, region, p):
                n = PIECE0 if region == 0 else PIECE
                at = piece_at(region, p, n)
                pool.wait_ge(split_hi, PIECES * unit + p + 1)
                pool.tensor_tensor(w_lo[:, at], w_raw[:, p, 0:n], w_hi[:, at].bitcast(F32), ALU.subtract
                                   ).then_inc(split_lo, 1)

            def batch(b, s, more):
                numerator(b, s)
                for p in range(PIECES):
                    if p == 2 and more:
                        rstd1(b + 1)
                    split(HALVES + b - 1, 2, p)
                rstd2(b)

            rstd1(0)
            split(0, 0, 0)
            rstd1(1)
            split(0, 0, 1)
            numerator(0, 0)
            split(0, 0, 2)
            split(0, 0, 3)
            split(1, 1, 0)
            split(1, 1, 1)
            rstd2(0)
            split(1, 1, 2)
            split(1, 1, 3)
            per0 = mk.k
            batch(1, 1, True)
            start2, per = mk.k, mk.k - per0
            with pool.Fori(0, 2) as i:
                mk.start(start2 + 2 * per * i)
                batch(2 * i + 2, 0, True)
                batch(2 * i + 3, 1, True)
                assert mk.k == 2 * per
            mk.start(start2 + 4 * per)
            batch(6, 0, True)
            batch(7, 1, False)
            for p in range(PIECES):
                split(UNITS - 1, 2, p)

            pool.wait_ge(idx_ready, 1)
            pool.wait_ge(xn_dma, 16 * B)
            pool.wait_ge(zero_dma, 16)

            def gather(s, k, par):
                if not isinstance(s, int) or s >= 2:
                    pool.wait_ge(xg_dma[par], 16 * k)
                pool.tensor_copy(gather_col[:, par:par + 1], idx_tab[:, 0, cols(s, 1)]).then_inc(idx_set, 1)
                pool.wait_ge(idx_set, s + 1)
                wait(pool, b_xt_done, s - 1)
                pool.sem_inc(pool_passed, 1)
                pool.indirect_dma_start(
                    xg[par], None, xn_dram[:, :],
                    bass.IndirectOffsetOnAxis(ap=gather_col[:, par:par + 1].bitcast(U32), axis=0)
                    ).then_inc(xg_dma[par], 16)

            def add(s, par):
                wait(pool, add_dma, 16 * s)
                pool.tensor_copy(add_col[:, par:par + 1], idx_tab[:, 1, cols(s, 1)]).then_inc(add_set, 1)
                pool.wait_ge(add_set, s + 1)
                pool.wait_ge(ys_ready, s + 1)
                pool.sem_inc(pool_passed, 1)
                pool.indirect_dma_start(
                    out[:, :], bass.IndirectOffsetOnAxis(ap=add_col[:, par:par + 1].bitcast(U32), axis=0),
                    ys[par], None, compute_op=ALU.add).then_inc(add_dma, 16)

            gather(0, 0, 0)
            gather(1, 0, 1)
            for par in range(2):
                pool.wait_ge(base_dma[par], 16 * TILES // 2)
            gather(2, 1, 0)
            gather(3, 1, 1)
            add(0, 0)
            with pool.Fori(1, (STEPS - 3) // 2) as i:
                for par in range(2):
                    gather(2 * i + par + 2, i + 1, par)
                    add(2 * i + par - 1, 1 - par)
            gather(STEPS - 1, STEPS // 2, 0)
            add(STEPS - 4, 1)
            add(STEPS - 3, 0)
            add(STEPS - 2, 1)
            add(STEPS - 1, 0)
            pool.wait_ge(add_dma, 16 * STEPS)

        @block.scalar
        def _(act):
            def split(unit, region, p, k):
                n = PIECE0 if region == 0 else PIECE
                at = piece_at(region, p, n)
                act.wait_ge(raw_dma[p], 16 * k)
                if region == 2 and not (isinstance(unit, int) and unit <= HALVES):
                    act.wait_ge(split_dma[p], 32 * (unit - HALVES))
                act.activation(w_hi[:, at], w_raw[:, p, 0:n], ACT.Copy).then_inc(split_hi, 1)

            def part_exp(b, k, s):
                wait(act, y_ready, 2 * b)
                key = [ky[:, c // 2, (c % 2) * T:(c % 2) * T + T] for c in range(CT)]
                for h in range(2):
                    wait(act, k_done, 2 * b + h + 1)
                    for c in (2 * h, 2 * h + 1):
                        last = act.activation(e2[:, c, :], key[c], ACT.Exp, bias=state_log[:, c:c + 1])
                    last.then_inc(e2_ready, 1)
                for c in range(CT):
                    last = act.activation(own[:, c, :], key[c], ACT.Exp, bias=own_log[:, c:c + 1])
                last.then_inc(own_ready, 1)

            def unit(n, u, tile=None, between=None):
                par = u % 2
                wait(act, g_done, n + 1)
                wait(act, h_ready, n - 1)
                if tile is not None and u % HALVES == 0:
                    act.activation(score.rearrange("p t e -> p (t e)")[:, cols(tile * E, E)],
                                   g_ps[:, H:H + E], ACT.Copy)
                act.activation(silu_g[:, par, :], g_ps[:, 0:H], ACT.Silu).then_inc(silu_ready, 1)
                if between is not None:
                    split(*between)
                wait(act, ht_done, n + 1)
                wait(act, down_done, n - 1)
                act.activation(h_hi[:, par, :, :].rearrange("p a t -> p (a t)"), ht_ps[:, 0:HC * P], ACT.Copy
                               ).then_inc(hhi_ready, 1)

            def part_x(b, k, s):
                for j in range(TJ):
                    wait(act, xt_done, 2 * b + j + 1)
                    wait(act, down_done, PER_BATCH * (b - 1))
                    act.activation(x_hi[:, s, j, :, :].rearrange("p a t -> p (a t)"), xt_ps[:, j, :], ACT.Copy
                                   ).then_inc(xhi_ready, 1)

            def batch(b, k, s, units):
                part_exp(b, k, s)
                for u in range(PER_BATCH):
                    unit(PER_BATCH * (b - 1) + u, u, 2 * (b - 1) + u // 2,
                         between=(HALVES + b - 1, 2, u, HALVES + b))
                part_x(b, k, s)

            act.wait_ge(dve_const, 1)
            act.activation(decay[:, :], decay[:, :], ACT.Exp).then_inc(act_mk, 1)
            split(0, 0, 0, 1)
            split(0, 0, 1, 1)
            part_exp(0, 0, 0)
            split(0, 0, 2, 1)
            split(0, 0, 3, 1)
            split(1, 1, 0, 2)
            split(1, 1, 1, 2)
            part_x(0, 0, 0)
            split(1, 1, 2, 2)
            split(1, 1, 3, 2)
            batch(1, 0, 1, PER_BATCH)
            with act.Fori(0, 2) as i:
                batch(2 * i + 2, i + 1, 0, PER_BATCH)
                batch(2 * i + 3, i + 1, 1, PER_BATCH)
            batch(6, 3, 0, PER_BATCH)
            batch(7, 3, 1, PER_BATCH)
            act.wait_ge(logit_done, 1)
            act.activation(score.rearrange("p t e -> p (t e)")[:, (TILES - TJ) * E:TILES * E], logit_ps, ACT.Copy
                           ).then_inc(score_ready, 1)
            act.wait_ge(score_ready, 1)
            act.activation(score[:, :, :], score[:, :, :], ACT.Exp, scale=-1.0).then_inc(score_ready, 1)
            for u in range(PER_BATCH):
                unit(PER_BATCH * (B - 1) + u, u, between=(UNITS - 1, 2, u, UNITS))

            def turned(s, par):
                wait(act, b_xt_done, s + 1)
                wait(act, b_u_done, s - 1)
                act.activation(x_hi[:, par, 0, :, :].rearrange("p a t -> p (a t)"), xt_ps[:, par, :], ACT.Copy
                               ).then_inc(b_xhi_ready, 1)

            def gate(s, par):
                wait(act, b_g_done, s + 1)
                wait(act, b_h_ready, s - 1)
                act.activation(silu_g[:, par, :], g_ps[:, 0:H], ACT.Silu).then_inc(b_silu_ready, 1)

            def hidden(s, par):
                wait(act, b_turn_done, s + 1)
                wait(act, step_done, s)
                act.activation(h_hi[:, par, :, :].rearrange("p a t -> p (a t)"), ht_ps[:, 0:HC * P], ACT.Copy
                               ).then_inc(b_hhi_ready, 1)

            def result(s, par):
                wait(act, step_done, s + 2)
                wait(act, add_dma, 16 * (s - 1))
                act.activation(ys[par], d_ps[:, :], ACT.Copy, scale=w_slot[:, cols(s, 1)]).then_inc(ys_ready, 1)

            def pair(i):
                for par in (1, 0):
                    s = 2 * i + 2 - par
                    gate(s, par)
                    turned(s + 1, 1 - par)
                    result(s - 1, 1 - par)
                    hidden(s, par)

            act.wait_ge(idx_ready, 1)
            turned(0, 0)
            gate(0, 0)
            turned(1, 1)
            hidden(0, 0)
            pair(0)
            with act.Fori(1, (STEPS - 3) // 2) as i:
                pair(i)
            gate(STEPS - 2, 1)
            turned(STEPS - 1, 0)
            result(STEPS - 3, 0)
            hidden(STEPS - 2, 1)
            gate(STEPS - 1, 0)
            result(STEPS - 2, 1)
            hidden(STEPS - 1, 0)
            result(STEPS - 1, 0)

        @block.vector
        def _(dve):
            mk = Marks(dve, dve_mk)
            def moments_of(n, src):
                for j in range(TJ):
                    m = mk.mark(dve.bn_stats(stats[:, n, j, :], src[:, j, :]))
                mk.need(m)
                dve.sem_inc(dve_passed, 1)
                for j in range(TJ):
                    last = dve.bn_aggr(moments[:, n, j, :], stats[:, n, j, :])
                return last

            def key_moments(b, k, s):
                wait(dve, x_dma[s], 16 * (k + 1))
                moments_of(0, x_in[:, s]).then_inc(var1_ready, 1)

            def norm(dst, src, n):
                for j in range(TJ):
                    last = dve.tensor_scalar(dst[:, j, :], src[:, j, :], moments[:, n, j, 0:1], rstd[:, n, j:j + 1],
                                             ALU.subtract, ALU.mult)
                return last

            def keys(b, s):
                wait(dve, rstd1_ready, b + 1)
                wait(dve, k_done, 2 * b)
                norm(k_tok, x_in[:, s], 0).then_inc(ktok_ready, 1)

            def unit_h(n, u):
                par = u % 2
                wait(dve, u_done, n + 1)
                wait(dve, silu_ready, n + 1)
                wait(dve, ht_done, n - 1)
                dve.tensor_tensor(h_sb[:, par, 0:H], silu_g[:, par, :], u_ps[:, 0:H], ALU.mult
                                  ).then_inc(h_ready, 1)

            def unit_lo(n, u):
                par = u % 2
                wait(dve, hhi_ready, n + 1)
                dve.tensor_tensor(h_lo[:, par, :, :].rearrange("p a t -> p (a t)"), ht_ps[:, 0:HC * P],
                                  h_hi[:, par, :, :].rearrange("p a t -> p (a t)").bitcast(F32), ALU.subtract
                                  ).then_inc(hlo_ready, 1)

            def unit(n, u):
                unit_h(n, u)
                unit_lo(n, u)

            def add_base(n, j, s):
                wait(dve, down_done, n + 1)
                dve.tensor_tensor(x1[:, s, j, :], x1[:, s, j, :], d_ps[:, :], ALU.add).then_inc(base_ready, 1)

            def inverse(c):
                return dve.reciprocal(e2[:, c, :], own[:, c, :])

            def half(buf, h):
                return buf[:, 2 * h:2 * h + 2, :]

            def batch(b, k, s, units, more):
                n0 = PER_BATCH * (b - 1)
                wait(dve, v_dma[s], 16 * (k + 1))
                dve.tensor_copy(p_st[:, :, 0:1], v_in[:, s, :, 0:1])
                if not units:
                    key_moments(b + 1, k, 1 - s)
                for h in range(2):
                    wait(dve, e2_ready, 2 * b + h + 1)
                    m_ev = mk.mark(dve.tensor_tensor(half(ev, h), half(e2, h), v_in[:, s, 2 * h:2 * h + 2, :],
                                                     ALU.mult))
                mk.need(m_ev)
                dve.sem_inc(ev_ready, 1)
                if isinstance(b, int) and b == 0:
                    dve.wait_ge(zero_dma, 16)
                    dve.memset(q_st[:, :, 0:1], 1.0)
                wait(dve, num_ready, b)
                for c in range(CT):
                    scan = dve.tensor_tensor_scan(p_st[:, c, 1:T], decay[:, c:c + 1].broadcast_to([P, T - 1]),
                                                  ev[:, c, 0:T - 1], 0.0, ALU.mult, ALU.add)
                scan.then_inc(p_ready, 1)
                for c in range(CT):
                    m_scan = mk.mark(dve.tensor_tensor_scan(
                        q_st[:, c, 1:T], decay[:, c:c + 1].broadcast_to([P, T - 1]),
                        e2[:, c, 0:T - 1], 0.0, ALU.mult, ALU.add))
                if units:
                    unit_h(n0, 0)
                else:
                    keys(b + 1, 1 - s)
                wait(dve, own_ready, b + 1)
                wait(dve, own_used, b + 1)
                mk.need(m_scan)
                for h in range(2):
                    m_den = mk.mark(dve.tensor_tensor(half(own, h), half(q_st, h), half(own, h), ALU.add))
                if units:
                    unit_lo(n0, 0)
                    if not isinstance(b, int) or b >= 2:
                        add_base(n0 - 1, 1, s)
                mk.need(m_den)
                inverse(0)
                inverse(1)
                if units:
                    unit_h(n0 + 1, 1)
                inverse(2)
                if units:
                    unit_lo(n0 + 1, 1)
                m_rec = mk.mark(inverse(3))
                wait(dve, num_ready, b + 1)
                mk.need(m_rec)
                for h in range(2):
                    dve.tensor_tensor(half(ev, h), half(ev, h), half(e2, h), ALU.mult).then_inc(y_ready, 1)
                if units:
                    unit_h(n0 + 2, 2)
                if more and units:
                    key_moments(b + 1, k if s == 0 else k + 1, 1 - s)
                if units:
                    unit_lo(n0 + 2, 2)
                    add_base(n0 + 1, 0, 1 - s)
                if more and units:
                    keys(b + 1, 1 - s)
                wait(dve, y_done, b + 1)
                if not isinstance(b, int) or b >= 2:
                    dve.wait_ge(base_dma[s], 32 * k)
                m_x1 = mk.mark(dve.tensor_tensor(x1[:, s, :, :], x_in[:, s, :, :], ky[:, :, :], ALU.add))
                mk.need(m_x1)
                dve.sem_inc(x1_ready, 1)
                moments_of(1, x1[:, s]).then_inc(var2_ready, 1)
                if units:
                    unit_h(n0 + 3, 3)
                wait(dve, rstd2_ready, b + 1)
                wait(dve, xn_dma, 16 * b)
                wait(dve, xt_done, 2 * b)
                norm(xn, x1[:, s], 1).then_inc(xn_ready, 1)
                if units:
                    unit_lo(n0 + 3, 3)
                for j in range(TJ):
                    wait(dve, xhi_ready, 2 * b + j + 1)
                    dve.tensor_tensor(x_lo[:, s, j, :, :].rearrange("p a t -> p (a t)"), xt_ps[:, j, :],
                                      x_hi[:, s, j, :, :].rearrange("p a t -> p (a t)").bitcast(F32),
                                      ALU.subtract).then_inc(xlo_ready, 1)

            key_moments(0, 0, 0)
            dve.wait_ge(const_in, 16 * N_CONST)
            a = mk.mark(dve.tensor_scalar(lift[:, :], w_ch[:, :], 0.0, None, ALU.max))
            dve.tensor_scalar(decay[:, :], w_ch[:, :], 0.0, None, ALU.min)
            mk.need(a)
            a = mk.mark(dve.tensor_tensor(lift[:, :], lift[:, :], u_ch[:, :], ALU.add))
            mk.need(a)
            dve.tensor_scalar(own_log[:, :], lift[:, :], 0.0, None, ALU.min)
            dve.tensor_scalar(state_log[:, :], lift[:, :], 0.0, -1.0, ALU.max, ALU.mult).then_inc(dve_const, 1)
            dve.wait_ge(pool_const, 1)
            for row in (0, 32):
                c1 = mk.mark(dve.tensor_scalar(wrow[row:row + 1, :], wrow[row:row + 1, :], -1.0, 0.0,
                                               ALU.mult, ALU.min))
            mk.need(c1)
            for row in (0, 32):
                c2 = mk.mark(dve.tensor_copy(neg_w[row:row + 1, :], wrow[row:row + 1, :]))
            mk.need(c2)
            dve.tensor_tensor(neg_w[32:33, :], wrow[32:33, :], neg_w[32:33, :].bitcast(F32), ALU.subtract)
            for row in (0, 32):
                dve.tensor_copy(ramp[row:row + 1, :], iota_i[row:row + 1, :])
            mk.mark(dve.tensor_copy(iota_f[:, :], iota_i[:, :]))
            dve.memset(ones8[:, :], 1.0).then_inc(dve_const, 1)
            keys(0, 0)
            dve.wait_ge(act_mk, 1)
            batch(0, 0, 0, False, True)
            per0 = mk.k
            batch(1, 0, 1, True, True)
            start2, per = mk.k, mk.k - per0
            with dve.Fori(0, 2) as i:
                mk.start(start2 + 2 * per * i)
                batch(2 * i + 2, i + 1, 0, True, True)
                batch(2 * i + 3, i + 1, 1, True, True)
                assert mk.k == 2 * per
            mk.start(start2 + 4 * per)
            batch(6, 3, 0, True, True)
            batch(7, 3, 1, True, False)

            def bc(ap, dim, n):
                shape = list(ap.shape)
                shape.insert(dim, n)
                return ap.unsqueeze(dim).broadcast_to(shape)

            def chain(ins):
                mk.need(mk.mark(ins))

            def scores():
                dve.wait_ge(score_ready, 2)
                chain(dve.tensor_scalar(score[:, :, :], score[:, :, :], 1.0, None, ALU.add))
                chain(dve.reciprocal(score[:, :, :], score[:, :, :]))
                chain(dve.tensor_tensor(biased[:, :, :], score[:, :, :], bc(bias_sb[:, :], 1, TILES), ALU.add))
                for t in range(TILES):
                    m = mk.mark(dve.max(top_v[:, t, :], biased[:, t, :]))
                mk.need(m)
                for t in range(TILES):
                    m = mk.mark(dve.max_index(top_i[:, t, :], top_v[:, t, :], biased[:, t, :]))
                mk.need(m)
                chain(dve.tensor_copy(top_f[:, :, :], top_i[:, :, 0:TOPK]))

            def choose():
                for k in range(TOPK):
                    m = mk.mark(dve.tensor_tensor(onehot[:, :, k, :], bc(iota_f[:, 0:E], 1, TILES),
                                                  bc(top_f[:, :, k], 2, E), ALU.is_equal))
                mk.need(m)
                chain(dve.tensor_tensor(chosen.rearrange("p e t -> p t e"), onehot[:, :, 0, :],
                                        onehot[:, :, 1, :], ALU.add))
                chain(dve.memset(first0[:, :, :], 1.0))
                chain(dve.memset(first0[:, :, 0:1], 0.0))
                flat = lambda ap: ap.rearrange("p e t -> p (e t)")
                dve.tensor_copy(chosen_b[:, :], flat(chosen[:, :, :]))
                chain(dve.tensor_tensor_scan(flat(upto[:, :, :]), flat(first0[:, :, :]), flat(chosen[:, :, :]),
                                             0.0, ALU.mult, ALU.add))
                dve.tensor_copy(total_b[:, :], upto[:, :, TILES - 1])
                dve.memset(ones_b[:, :], 1.0)
                dve.tensor_copy(row_id[:, :], row_ii[:, :])
                dve.tensor_scalar(row_id1[:, :], row_ii[:, :], 1.0, None, ALU.add)
                dve.tensor_scalar(dump, row_ii[:, :], float(B * T + 1), None, ALU.add)
                chain(dve.tensor_tensor(before_b[:, :], flat(upto[:, :, :]), flat(chosen[:, :, :]), ALU.subtract))
                dve.tensor_scalar(tri[:, :], iota_f[:, 0:P], row_id[:, 0:1], None, ALU.is_gt
                                  ).then_inc(chosen_ready, 1)

            def gates():
                for k in range(TOPK):
                    m = mk.mark(dve.tensor_tensor(picked[:, :, k, :], onehot[:, :, k, :], score[:, :, :], ALU.mult))
                mk.need(m)
                chain(dve.reduce_sum(w_top[:, :, :], picked[:, :, :, :], AX.X))
                chain(dve.tensor_tensor(w_sum[:, :], w_top[:, :, 0], w_top[:, :, 1], ALU.add))
                chain(dve.reciprocal(w_sum[:, :], w_sum[:, :]))
                dve.tensor_tensor(w_tok[:, :, :], w_top[:, :, :], bc(w_sum[:, :], 2, TOPK), ALU.mult)
                dve.tensor_scalar(token_id[:, :], iota_f[:, 0:TILES], float(P), row_id1[:, 0:1], ALU.mult, ALU.add)

            def places():
                dve.wait_ge(rank_done, 1)
                chain(dve.tensor_scalar(n_i[:, :], count_ps, float(P - 1), None, ALU.add))
                chain(dve.tensor_scalar(n_i[:, :], n_i[:, :], 7, None, ALU.logical_shift_right))
                chain(dve.tensor_copy(n_tiles[:, :], n_i[:, :]))
                chain(dve.tensor_tensor_scan(ends[:, :], ones8[:, :], n_tiles[:, :], 0.0, ALU.mult, ALU.add))
                chain(dve.tensor_tensor(starts[:, :], ends[:, :], n_tiles[:, :], ALU.subtract))
                chain(dve.scalar_tensor_tensor(place[:, :, :], bc(starts[:, :], 2, TILES), float(P),
                                               rank_ps.rearrange("p (e t) -> p e t", e=E), ALU.mult, ALU.add))
                for k in range(TOPK):
                    m = mk.mark(dve.tensor_tensor(picked[:, :, k, :], onehot[:, :, k, :],
                                                  place.rearrange("p e t -> p t e"), ALU.mult))
                mk.need(m)
                chain(dve.reduce_sum(slot_f[:, :, :], picked[:, :, :, :], AX.X))
                chain(dve.tensor_copy(slot_i[:, :, :], slot_f[:, :, :]))
                dve.tensor_scalar(part_i[:, 0, :, :], slot_i[:, :, :], P - 1, None, ALU.bitwise_and)
                chain(dve.tensor_scalar(part_i[:, 1, :, :], slot_i[:, :, :], 7, None, ALU.logical_shift_right))
                chain(dve.tensor_copy(part_f[:, :, :, :], part_i[:, :, :, :]))
                for t in range(TILES):
                    for k in range(TOPK):
                        n = t * TOPK + k
                        wait(dve, onehot_used, n - 3)
                        at = part_f[:, 1, t, k:k + 1]
                        dve.tensor_scalar(at_row[:, n % 4, :], iota_f[:, 0:P], part_f[:, 0, t, k:k + 1], None,
                                          ALU.is_equal)
                        dve.tensor_scalar(at_step[:, n % 4, 0, :], iota_f[:, 0:STEPS_PAD], at,
                                          token_id[:, t:t + 1], ALU.is_equal, ALU.mult)
                        dve.tensor_scalar(at_step[:, n % 4, 1, :], iota_f[:, 0:STEPS_PAD], at,
                                          w_tok[:, t, k:k + 1], ALU.is_equal, ALU.mult
                                          ).then_inc(onehot_ready, 1)

            def steps():
                chain(dve.tensor_tensor(past[:, :, :], bc(iota_f[:, 0:STEPS_PAD], 1, E - 1),
                                        bc(ends[:, 0:E - 1], 2, STEPS_PAD), ALU.is_ge))
                chain(dve.reduce_sum(of_step[:, :], past.rearrange("p e s -> p s e"), AX.X))
                dve.tensor_scalar(w_need[:, :], of_step[:, :], 1.0, None, ALU.add)
                chain(dve.tensor_scalar(w_off_f[:, :], of_step[:, :], float(HALVES), None, ALU.add))
                for e in range(0, E - 1, 3):
                    chain(dve.scalar_tensor_tensor(w_off_f[:, :], past[:, e, :], -3.0, w_off_f[:, :],
                                                   ALU.mult, ALU.add))
                chain(dve.tensor_scalar(slot_no, w_off_f[:, :], 0.5, float(WCOLS0 - WCOLS), ALU.is_gt, ALU.mult))
                dve.scalar_tensor_tensor(w_off[:, :], w_off_f[:, :], float(WCOLS), slot_no, ALU.mult, ALU.add)
                chain(dve.tensor_scalar(ends_i[:, :], ends[:, :], 1.0, None, ALU.add))
                dve.nop().then_inc(steps_ready, 1)
                dve.wait_ge(onehot_used, TILES * TOPK)
                chain(dve.tensor_copy(slot_v, table_ps[:, 0:STEPS_PAD]))
                dve.tensor_copy(w_slot[:, :], table_ps[:, STEPS_PAD:2 * STEPS_PAD])
                dve.tensor_scalar(idx_tab[:, 0, :], slot_v, -1.0, 0.0, ALU.add, ALU.max)
                chain(dve.tensor_scalar(slot_no, slot_v, 0.0, dump, ALU.is_equal, ALU.mult))
                dve.scalar_tensor_tensor(idx_tab[:, 1, :], slot_v, -1.0, slot_no, ALU.add, ALU.add
                                         ).then_inc(idx_ready, 1)

            n7 = PER_BATCH * (B - 1)
            unit(n7, 0)
            add_base(n7 - 1, 1, 0)
            scores()
            unit(n7 + 1, 1)
            choose()
            unit(n7 + 2, 2)
            add_base(n7 + 1, 0, 1)
            gates()
            unit(n7 + 3, 3)
            places()
            steps()
            add_base(n7 + 3, 1, 1)

            def turned(s, par):
                wait(dve, b_xhi_ready, s + 1)
                dve.tensor_tensor(x_lo[:, par, 0, :, :].rearrange("p a t -> p (a t)"), xt_ps[:, par, :],
                                  x_hi[:, par, 0, :, :].rearrange("p a t -> p (a t)").bitcast(F32),
                                  ALU.subtract).then_inc(b_xlo_ready, 1)

            def hidden(s, par):
                wait(dve, b_u_done, s + 1)
                wait(dve, b_silu_ready, s + 1)
                wait(dve, b_turn_done, s - 1)
                dve.tensor_tensor(h_sb[:, par, 0:H], silu_g[:, par, :], u_ps[:, 0:H], ALU.mult
                                  ).then_inc(b_h_ready, 1)

            def hidden_lo(s, par):
                wait(dve, b_hhi_ready, s + 1)
                dve.tensor_tensor(h_lo[:, par, :, :].rearrange("p a t -> p (a t)"), ht_ps[:, 0:HC * P],
                                  h_hi[:, par, :, :].rearrange("p a t -> p (a t)").bitcast(F32), ALU.subtract
                                  ).then_inc(b_hlo_ready, 1)

            def step(s, par, more):
                hidden(s, par)
                if more:
                    turned(s + 1, 1 - par)
                hidden_lo(s, par)

            turned(0, 0)
            step(0, 0, True)
            step(1, 1, True)
            step(2, 0, True)
            with dve.Fori(1, (STEPS - 3) // 2) as i:
                step(2 * i + 1, 1, True)
                step(2 * i + 2, 0, True)
            step(STEPS - 2, 1, True)
            step(STEPS - 1, 0, False)

        @block.tensor
        def _(pe):
            def keys(b, halves):
                wait(pe, ktok_ready, b + 1)
                wait(pe, x1_ready, b)
                for h in halves:
                    for c in (2 * h, 2 * h + 1):
                        region = ky[:, h, (c % 2) * T:(c % 2) * T + T]
                        pe.matmul(region, neg_w[:, c * P:(c + 1) * P], ramp[:, :], start=True, stop=False)
                        for j in range(TJ):
                            last = pe.matmul(region[:, j * P:(j + 1) * P], k_tok[:, j, c * P:(c + 1) * P],
                                             ident[:, :], start=False, stop=(j == TJ - 1))
                    last.then_inc(k_done, 1)

            def y_turn(b):
                for h in range(2):
                    wait(pe, y_ready, 2 * b + h + 1)
                    for j in range(TJ):
                        for c in (2 * h, 2 * h + 1):
                            last = pe.transpose(ky[:, j, c * P:(c + 1) * P], ev[:, c, j * P:(j + 1) * P],
                                                ident[:, :])
                last.then_inc(y_done, 1)

            def x_turn(b):
                wait(pe, xn_ready, b + 1)
                wait(pe, xlo_ready, 2 * b)
                for j in range(TJ):
                    for c in range(CT):
                        last = pe.transpose(xt_ps[:, j, c * P:(c + 1) * P], xn[:, j, c * P:(c + 1) * P],
                                            ident[:, :])
                    last.then_inc(xt_done, 1)

            def product(dst, pairs, first=True, final=True):
                n = len(pairs)
                for i, (a_hi, a_lo, b_hi, b_lo) in enumerate(pairs):
                    pe.matmul(dst, a_hi, b_hi, start=(first and i == 0), stop=False)
                    pe.matmul(dst, a_hi, b_lo, start=False, stop=False)
                    last = pe.matmul(dst, a_lo, b_hi, start=False, stop=(final and i == n - 1))
                return last

            def logits(b, s):
                wait(pe, xlo_ready, 2 * b + 2)
                wait(pe, hlo_ready, PER_BATCH * b)
                at = [slice(c * UP0 + H, c * UP0 + H + E) for c in range(CT)]
                for j in range(TJ):
                    last = product(logit_ps[:, j * E:(j + 1) * E],
                                   [(x_hi[:, s, j, c, :], x_lo[:, s, j, c, :], w_hi[:, at[c]], w_lo[:, at[c]])
                                    for c in range(CT)])
                last.then_inc(logit_done, 1)

            def unit(n, u, s, logit_batches=None, first=False):
                j, half, par = u // HALVES, u % HALVES, u % 2
                if isinstance(n, int) and n == 1:
                    pe.wait_ge(split_lo, PIECES * HALVES)
                if u == 0:
                    wait(pe, xlo_ready, (n + PER_BATCH) // 2 if isinstance(n, int) else logit_batches * 2)
                wait(pe, silu_ready, n)
                width = UP0 if half == 0 else UP
                at = REGION_AT[half]
                for bank, off, n_cols, free, done in (
                        (g_ps, 0, width - H, None, g_done), (u_ps, width - H, H, h_ready, u_done)):
                    if free is not None:
                        wait(pe, free, n)
                    part = [slice(at + c * width + off, at + c * width + off + n_cols) for c in range(CT)]
                    product(bank[:, 0:n_cols],
                            [(x_hi[:, s, j, c, :], x_lo[:, s, j, c, :], w_hi[:, part[c]], w_lo[:, part[c]])
                             for c in range(CT)]).then_inc(done, 1)
                if not first:
                    down(n - 1, (u - 1) % HALVES)
                if isinstance(n, int) and n == PER_BATCH * (B - 1):
                    pe.wait_ge(score_ready, 1)
                wait(pe, h_ready, n + 1)
                for c in range(HC):
                    last = pe.transpose(ht_ps[:, c * P:(c + 1) * P], h_sb[:, par, c * P:(c + 1) * P], ident[:, :])
                last.then_inc(ht_done, 1)

            def down(n, half):
                wait(pe, hlo_ready, n + 1)
                if half == 0:
                    tile = (n // 2) if isinstance(n, int) else None
                    wait(pe, base_ready, tile if tile is not None else down_tile[0])
                at = REGION_AT[half] + CT * (UP0 if half == 0 else UP)
                part = [slice(at + c * C, at + (c + 1) * C) for c in range(HC)]
                product(d_ps[:, :],
                        [(h_hi[:, half, c, :], h_lo[:, half, c, :], w_hi[:, part[c]], w_lo[:, part[c]])
                         for c in range(HC)],
                        first=(half == 0), final=(half == 1)).then_inc(down_done, 1)

            down_tile = [None]

            def batch(b, s, units, more):
                n0 = PER_BATCH * (b - 1)
                for u in range(units):
                    if u == 3:
                        y_turn(b)
                    down_tile[0] = 2 * (b - 1) + (u - 1) // 2
                    unit(n0 + u, u, 1 - s, b, first=(isinstance(b, int) and b == 1 and u == 0))
                if not units:
                    y_turn(b)
                if more:
                    keys(b + 1, (0,))
                x_turn(b)
                if more:
                    keys(b + 1, (1,))
                else:
                    logits(b, s)

            pe.wait_ge(pool_const, 1)
            pe.wait_ge(zeros_ready, 1)
            pe.wait_ge(dve_const, 2)
            keys(0, (0, 1))
            batch(0, 0, 0, True)
            pe.wait_ge(split_lo, PIECES)
            batch(1, 1, PER_BATCH, True)
            with pe.Fori(0, 2) as i:
                batch(2 * i + 2, 0, PER_BATCH, True)
                batch(2 * i + 3, 1, PER_BATCH, True)
            batch(6, 0, PER_BATCH, True)
            batch(7, 1, PER_BATCH, False)

            n7 = PER_BATCH * (B - 1)
            for u in range(PER_BATCH):
                down_tile[0] = 2 * (B - 1) + (u - 1) // 2
                unit(n7 + u, u, 1, B)
                if u == 1:
                    pe.wait_ge(chosen_ready, 1)
                    pe.matmul(rank_ps, tri[:, :], chosen_b[:, :], start=True, stop=False)
                    pe.matmul(rank_ps, ones_b[:, :], before_b[:, :], start=False, stop=True)
                    pe.matmul(count_ps, ones_b[:, :], total_b[:, :], start=True, stop=True
                              ).then_inc(rank_done, 1)
            down(n7 + PER_BATCH - 1, 1)
            for n in range(TILES * TOPK):
                pe.wait_ge(onehot_ready, n + 1)
                pe.matmul(table_ps, at_row[:, n % 4, :], at_step[:, n % 4, :, :].rearrange("p a s -> p (a s)"), start=(n == 0),
                          stop=(n == TILES * TOPK - 1)).then_inc(onehot_used, 1)

            def turn_x(s, k, par):
                wait(pe, xg_dma[par], 16 * (k + 1))
                wait(pe, b_xlo_ready, s - 1)
                for c in range(CT):
                    last = pe.transpose(xt_ps[:, par, c * P:(c + 1) * P], xg[par][:, c * P:(c + 1) * P],
                                        ident[:, :])
                last.then_inc(b_xt_done, 1)

            def up(s, par):
                need = pe.value_load(w_need[0:1, cols(s, 1)], min_val=1, max_val=E)
                off = pe.value_load(w_off[0:1, cols(s, 1)], min_val=0, max_val=REGION_AT[2])
                pe.wait_ge(w_ready, need)
                wait(pe, b_xlo_ready, s + 1)
                wait(pe, b_silu_ready, s)
                for bank, o, free, done in ((g_ps, 0, None, b_g_done), (u_ps, H, b_h_ready, b_u_done)):
                    if free is not None:
                        wait(pe, free, s)
                    product(bank[:, 0:H],
                            [(x_hi[:, par, 0, c, :], x_lo[:, par, 0, c, :],
                              w_hi[:, bass.DynSlice(off + (c * UP + o), H)],
                              w_lo[:, bass.DynSlice(off + (c * UP + o), H)]) for c in range(CT)]
                            ).then_inc(done, 1)

            def down_step(s, par):
                off = pe.value_load(w_off[0:1, cols(s, 1)], min_val=0, max_val=REGION_AT[2])
                wait(pe, b_hlo_ready, s + 1)
                wait(pe, ys_ready, s)
                product(d_ps[:, :],
                        [(h_hi[:, par, c, :], h_lo[:, par, c, :],
                          w_hi[:, bass.DynSlice(off + (DOWN0 + c * C), C)],
                          w_lo[:, bass.DynSlice(off + (DOWN0 + c * C), C)]) for c in range(HC)]
                        ).then_inc(step_done, 1)

            def turn_h(s, par):
                wait(pe, b_h_ready, s + 1)
                wait(pe, b_hlo_ready, s)
                for c in range(HC):
                    last = pe.transpose(ht_ps[:, c * P:(c + 1) * P], h_sb[:, par, c * P:(c + 1) * P], ident[:, :])
                last.then_inc(b_turn_done, 1)

            pe.wait_ge(steps_ready, 1)
            pe.wait_ge(idx_ready, 1)
            pe.wait_ge(base_ready, TILES)
            pe.nop().then_inc(step_done, 1)
            turn_x(0, 0, 0)
            up(0, 0)
            turn_x(1, 0, 1)
            turn_h(0, 0)

            def pair(i):
                for par in (1, 0):
                    s = 2 * i + 2 - par
                    up(s, par)
                    turn_x(s + 1, i + 1, 1 - par)
                    down_step(s - 1, 1 - par)
                    turn_h(s, par)

            pair(0)
            with pe.Fori(1, (STEPS - 3) // 2) as i:
                pair(i)
            up(STEPS - 2, 1)
            turn_x(STEPS - 1, (STEPS - 1) // 2, 0)
            down_step(STEPS - 3, 0)
            turn_h(STEPS - 2, 1)
            up(STEPS - 1, 0)
            down_step(STEPS - 2, 1)
            turn_h(STEPS - 1, 0)
            down_step(STEPS - 1, 0)


def kernel(**inputs):
    import numpy as np
    from concourse import bacc
    from concourse import mybir as mb
    from concourse.bass_utils import run_bass_kernel_spmd as run

    a = {k: np.asarray(v) for k, v in inputs.items()}
    hs = HALVES * H

    def unit(up, down):
        w = np.zeros((P, WCOLS0), np.float32)
        n = CT * up.shape[0]
        w[:, :n] = up.T.reshape(CT, P, up.shape[0]).transpose(1, 0, 2).reshape(P, n)
        d = np.zeros((HC * P, C), np.float32)
        d[:H] = down.T
        w[:, n:n + HC * C] = d.reshape(HC, P, C).transpose(1, 0, 2).reshape(P, HC * C)
        return w

    sg, sd = a["L0_ffn_shared_gw"], a["L0_ffn_shared_dw"]
    router = [a["L0_ffn_gate_w"], a["L0_ffn_gate_w"][:0]]
    units = [unit(np.concatenate([sg[hs + h * H:hs + (h + 1) * H], router[h], sg[h * H:(h + 1) * H]]),
                  sd[:, h * H:(h + 1) * H]) for h in range(HALVES)]
    units += [unit(a["L0_ffn_up_w"][e], a["L0_ffn_down_w"][e]) for e in reversed(range(E))]
    arrays = {
        "x_in_dram": np.ascontiguousarray(a["x"]).reshape(B * T, C),
        "ctx_t_dram": np.ascontiguousarray(a["ctx_2048"].transpose(0, 2, 1)).reshape(B * C, T),
        "w_row_dram": np.ascontiguousarray(a["L0_xattn_w"]).reshape(1, C),
        "wu_ch_dram": np.concatenate([a[n].reshape(CT, P).T for n in ("L0_xattn_w", "L0_xattn_u")], axis=1),
        "bias_dram": np.ascontiguousarray(np.broadcast_to(a["L0_ffn_gate_bias"], (P, E))),
        "weights_dram": np.concatenate(units),
    }
    nc = bacc.Bacc("TRN2", target_bir_lowering=False, num_devices=1)
    args = [nc.dram_tensor(n, v.shape, mb.dt.float32, kind="ExternalInput").ap() for n, v in arrays.items()]
    args.append(nc.dram_tensor("xn_scratch", (B * T, C), mb.dt.float32).ap())
    for part in ("hi", "lo"):
        args.append(nc.dram_tensor(f"w_{part}_scratch", (E * P, WCOLS), mb.dt.float32).ap())
    args.append(nc.dram_tensor("out_dram", (B * T + SPARE_ROWS, C), mb.dt.float32, kind="ExternalOutput").ap())
    build(nc, *args)
    r = run(nc, [arrays], core_ids=[0])
    return r.results[0]["out_dram"][:B * T].reshape(B, T, C)
```

```python
import concourse.bass as bass
from concourse import mybir
from contextlib import ExitStack

F32 = mybir.dt.float32
F32R = mybir.dt.float32r
BF16 = mybir.dt.bfloat16
I32 = mybir.dt.int32
U32 = mybir.dt.uint32
ALU = mybir.AluOpType
ACT = mybir.ActivationFunctionType
AX = mybir.AxisListType

P = 128
B, T, C = 8, 256, 512
CT = C // P
TJ = T // P
TILES = B * TJ
E, TOPK = 8, 2
H = 352
HALVES = 2
HC = 3
UP = 2 * H
WCOLS = CT * UP + HC * C
DOWN0 = CT * UP
UP0 = UP + E
WCOLS0 = CT * UP0 + HC * C
REGION_AT = [0, WCOLS0, WCOLS0 + WCOLS]
STEPS = TILES * TOPK + E - 1
STEPS_PAD = STEPS + 1
UNITS = HALVES + E
REGIONS = 3
PIECES = 4
PIECE = WCOLS // PIECES
PIECE0 = WCOLS0 // PIECES
SPARE_ROWS = P
GROUP = 8
GROUPS = TILES * TOPK // GROUP
STEP_COLS = GROUP * 2 * STEPS_PAD
EARLY = TILES - 2 * TJ
PER_BATCH = TJ * HALVES
EPS = 1e-5


class Marks:

    def __init__(self, eng, sem):
        self.eng, self.sem, self.base, self.k = eng, sem, 0, 0

    def start(self, base):
        self.base, self.k = base, 0

    def mark(self, ins):
        self.k += 1
        ins.then_inc(self.sem, 1)
        return self.base + self.k

    def need(self, mark):
        self.eng.wait_ge(self.sem, mark)


def wait(eng, sem, value):
    if isinstance(value, int) and value <= 0:
        return
    eng.wait_ge(sem, value)


def piece_at(region, p, n=PIECE):
    return slice(REGION_AT[region] + p * n, REGION_AT[region] + (p + 1) * n)


def cols(start, n):
    return slice(start, start + n) if isinstance(start, int) else bass.DynSlice(start, n)


def build(nc, x, ctx_t, w_row, wu_ch, bias, weights, xn_dram, hi_dram, lo_dram, out):
    with ExitStack() as ctx:
        def sb(name, shape, dt=F32):
            return ctx.enter_context(nc.sbuf_tensor(name, shape, dt))

        def pb(name, shape, dt=F32):
            return ctx.enter_context(nc.psum_tensor(name, shape, dt))

        def sem(name):
            return ctx.enter_context(nc.semaphore(name))

        w_hi = sb("w_hi", [P, WCOLS0 + 2 * WCOLS], F32R)
        w_lo = sb("w_lo", [P, WCOLS0 + 2 * WCOLS], F32R)
        w_raw = sb("w_raw", [P, PIECES, PIECE0])
        ident = sb("ident", [P, P])
        ramp = sb("ramp", [P, T], F32R)
        neg_w = sb("neg_w", [P, C], F32R)
        iota_f = sb("iota_f", [P, T])
        row_id = sb("row_id", [P, 1])
        row_id1 = sb("row_id1", [P, 1])
        row_ii = sb("row_ii", [P, 1], I32)
        token_id = sb("token_id", [P, TILES, TOPK])
        w_ch = sb("w_ch", [P, CT])
        u_ch = sb("u_ch", [P, CT])
        decay = sb("decay", [P, CT])
        state_log = sb("state_log", [P, CT])
        own_log = sb("own_log", [P, CT])
        lift = sb("lift", [P, CT])
        bias_sb = sb("bias_sb", [P, E])
        ones_b = sb("ones_b", [P, P], BF16)
        minus_half = sb("minus_half", [P, TJ])
        x_in = sb("x_in", [P, 2, TJ, C])
        v_in = sb("v_in", [P, 2, CT, T])
        k_tok = sb("k_tok", [P, TJ, C])
        stats = sb("stats", [P, 2, TJ, 6])
        moments = sb("moments", [P, 2, TJ, 2])
        rstd = sb("rstd", [P, 2, TJ])
        own = sb("own", [P, CT, T])
        e2 = sb("e2", [P, CT, T])
        ev = sb("ev", [P, CT, T])
        p_st = sb("p_st", [P, CT, T])
        q_st = sb("q_st", [P, CT, T])
        x1 = sb("x1", [P, 2, TJ, C])
        xn = sb("xn", [P, TJ, C])
        x_hi = sb("x_hi", [P, 2, TJ, CT, P], F32R)
        x_lo = sb("x_lo", [P, 2, TJ, CT, P], F32R)
        silu_g = sb("silu_g", [P, 2, H])
        h_sb = sb("h_sb", [P, 2, HC * P])
        h_hi = sb("h_hi", [P, 2, HC, P], F32R)
        h_lo = sb("h_lo", [P, 2, HC, P], F32R)
        score = sb("score", [P, TILES, E])
        top_f = sb("top_f", [P, TILES, TOPK])
        w_top = sb("w_top", [P, TILES, TOPK])
        w_tok = sb("w_tok", [P, TILES, TOPK])
        chosen_b = sb("chosen_b", [P, E * TILES], BF16)
        total_b = sb("total_b", [P, E], BF16)
        n_i = sb("n_i", [P, E], I32)
        n_tiles = sb("n_tiles", [P, E])
        ends = sb("ends", [P, E])
        starts = sb("starts", [P, E])
        ones8 = sb("ones8", [P, E])
        slot_f = sb("slot_f", [P, TILES, TOPK])
        slot_i = sb("slot_i", [P, TILES, TOPK], I32)
        part_i = sb("part_i", [P, 2, TILES, TOPK], I32)
        part_f = sb("part_f", [P, 2, TILES, TOPK])
        ends_i = sb("ends_i", [P, E], I32)
        spare_p = p_st.rearrange("p a t -> p (a t)")
        spare_q = q_st.rearrange("p a t -> p (a t)")
        onehot = spare_p[:, 0:256].rearrange("p (t k e) -> p t k e", t=TILES, k=TOPK)
        picked = spare_p[:, 256:512].rearrange("p (t k e) -> p t k e", t=TILES, k=TOPK)
        past = spare_p[:, 512:512 + (E - 1) * STEPS_PAD].rearrange("p (e s) -> p e s", e=E - 1)
        spare_x = x_in.rearrange("p s j c -> p (s j c)")
        biased = spare_x[:, 0:128].rearrange("p (t e) -> p t e", t=TILES)
        top_v = spare_x[:, 128:256].rearrange("p (t e) -> p t e", t=TILES)
        top_i = spare_x[:, 256:384].bitcast(U32).rearrange("p (t k) -> p t k", t=TILES)
        chosen = spare_q[:, 256:384].rearrange("p (e t) -> p e t", e=E)
        upto = spare_q[:, 384:512].rearrange("p (e t) -> p e t", e=E)
        place = spare_q[:, 512:640].rearrange("p (e t) -> p e t", e=E)
        first0 = spare_q[:, 640:768].rearrange("p (e t) -> p e t", e=E)
        of_step = spare_p[:, 792:792 + STEPS_PAD]
        w_off_f = spare_p[:, 832:832 + STEPS_PAD]
        spare_v = v_in.rearrange("p s a t -> p (s a t)")
        before_b = spare_v[:, 1296:1296 + E * TILES // 2].bitcast(BF16)
        w_sum = spare_v[:, 1392:1392 + TILES]
        slot_v = spare_v[:, 1408:1408 + STEPS_PAD]
        slot_no = spare_v[:, 1472:1472 + STEPS_PAD]
        dump = spare_v[:, 1536:1537]
        step_ints = e2.rearrange("p a t -> p (a t)").bitcast(I32)
        w_off = step_ints[:, 0:STEPS_PAD]
        w_need = step_ints[:, 64:64 + STEPS_PAD]
        idx_tab = step_ints[:, 128:128 + 2 * STEPS_PAD].rearrange("p (a s) -> p a s", a=2)
        w_slot = own.rearrange("p a t -> p (a t)")[:, 0:STEPS_PAD]
        tri = spare_q[:, 936:1000].bitcast(BF16)
        wrow = x1[:, 1, 0, :]
        iota_i = x1[:, 1, 1, 0:T].bitcast(I32)
        gather_col = sb("gather_col", [P, 2], I32)
        add_col = sb("add_col", [P, 2], I32)
        xg = [k_tok[:, j, :] for j in range(2)]
        ys = [ev[:, 2 * j:2 * j + 2, :].rearrange("p a t -> p (a t)") for j in range(2)]

        flat_ev, flat_k = (buf.rearrange("p a t -> p (a t)") for buf in (ev, k_tok))
        at_row = [ap.rearrange("p (n r) -> p n r", n=GROUP)
                  for ap in (spare_x[:, 0:GROUP * P], spare_x[:, GROUP * P:2 * GROUP * P], flat_ev)]
        at_step = [ap.rearrange("p (n a s) -> p n a s", n=GROUP, a=2)
                   for ap in (spare_v[:, 0:STEP_COLS], spare_v[:, STEP_COLS:2 * STEP_COLS], flat_k[:, 0:STEP_COLS])]
        is_step = own.rearrange("p a t -> p (a t)")[:, 64:64 + 2 * GROUP * STEPS_PAD].rearrange(
            "p (g n s) -> p g n s", g=2, n=GROUP)

        ky = pb("ky", [P, 2, C])
        xt_ps = pb("xt_ps", [P, 2, C])
        g_ps = pb("g_ps", [P, C])
        u_ps = pb("u_ps", [P, C])
        ht_ps = pb("ht_ps", [P, C])
        d_ps = pb("d_ps", [P, C])
        logit_ps = ht_ps[:, HC * P:HC * P + TJ * E]
        rank_ps = xt_ps[:, 0, 0:E * TILES]
        count_ps = xt_ps[:, 0, E * TILES:E * TILES + E]
        table_ps = xt_ps[:, 1, 0:2 * STEPS_PAD]

        const_in = sem("const_in")
        pool_mk = sem("pool_mk")
        dve_mk = sem("dve_mk")
        dve_passed = sem("dve_passed")
        pool_passed = sem("pool_passed")
        sp_passed = sem("sp_passed")
        act_mk = sem("act_mk")
        x_dma = [sem(f"x_dma{s}") for s in range(2)]
        v_dma = [sem(f"v_dma{s}") for s in range(2)]
        xn_dma = sem("xn_dma")
        base_dma = [sem(f"base_dma{s}") for s in range(2)]
        raw_dma = [sem(f"raw_dma{p}") for p in range(PIECES)]
        split_dma = [sem(f"split_dma{p}") for p in range(PIECES)]
        zero_dma = sem("zero_dma")
        region_dma = [sem(f"region_dma{p}") for p in range(2)]
        w_ready = sem("w_ready")
        pool_const = sem("pool_const")
        zeros_ready = sem("zeros_ready")
        dve_const = sem("dve_const")
        split_hi = sem("split_hi")
        split_lo = sem("split_lo")
        var1_ready = sem("var1_ready")
        ktok_ready = sem("ktok_ready")
        k_done = sem("k_done")
        rstd1_ready = sem("rstd1_ready")
        rstd2_ready = sem("rstd2_ready")
        e2_ready = sem("e2_ready")
        own_ready = sem("own_ready")
        ev_ready = sem("ev_ready")
        x1_ready = sem("x1_ready")
        p_ready = sem("p_ready")
        num_ready = sem("num_ready")
        y_ready = sem("y_ready")
        y_done = sem("y_done")
        var2_ready = sem("var2_ready")
        xn_ready = sem("xn_ready")
        xt_done = sem("xt_done")
        xhi_ready = sem("xhi_ready")
        xlo_ready = sem("xlo_ready")
        logit_done = sem("logit_done")
        logit_read = sem("logit_read")
        score_ready = sem("score_ready")
        g_done = sem("g_done")
        u_done = sem("u_done")
        silu_ready = sem("silu_ready")
        h_ready = sem("h_ready")
        ht_done = sem("ht_done")
        hhi_ready = sem("hhi_ready")
        hlo_ready = sem("hlo_ready")
        down_done = sem("down_done")
        base_ready = sem("base_ready")
        chosen_ready = sem("chosen_ready")
        rank_done = sem("rank_done")
        onehot_ready = sem("onehot_ready")
        onehot_used = sem("onehot_used")
        steps_ready = sem("steps_ready")
        idx_ready = sem("idx_ready")
        idx_set = sem("idx_set")
        xg_dma = [sem(f"xg_dma{s}") for s in range(2)]
        b_xt_done = sem("b_xt_done")
        b_xhi_ready = sem("b_xhi_ready")
        b_xlo_ready = sem("b_xlo_ready")
        b_g_done = sem("b_g_done")
        b_u_done = sem("b_u_done")
        b_silu_ready = sem("b_silu_ready")
        b_h_ready = sem("b_h_ready")
        b_turn_done = sem("b_turn_done")
        b_hhi_ready = sem("b_hhi_ready")
        b_hlo_ready = sem("b_hlo_ready")
        step_done = sem("step_done")
        ys_ready = sem("ys_ready")
        add_set = sem("add_set")
        add_dma = sem("add_dma")

        N_CONST = 5
        block = ctx.enter_context(nc.Block())

        @block.sync
        def _(sp):
            def load_x(b, s):
                sp.dma_start(x_in[:, s, :, :],
                             x[cols(b * T, T), :].rearrange("(j p) c -> p j c", p=P)).then_inc(x_dma[s], 16)

            def load_v(b, s):
                sp.dma_start(v_in[:, s, :, :],
                             ctx_t[cols(b * C, C), :].rearrange("(a p) t -> p a t", p=P)).then_inc(v_dma[s], 16)

            def load_piece(unit, p):
                wait(sp, split_lo, PIECES * (unit - 1) + p + 1)
                n = PIECE0 if isinstance(unit, int) and unit == 0 else PIECE
                sp.dma_start(w_raw[:, p, 0:n], weights[cols(unit * P, P), p * n:(p + 1) * n]
                             ).then_inc(raw_dma[p], 16)

            def store_base(t, j, s):
                sp.wait_ge(base_ready, t + 1)
                sp.dma_start(out[cols(t * P, P), :], x1[:, s, j, :]).then_inc(base_dma[s], 16)

            def store_piece(b, p):
                at = piece_at(2, p)
                sp.wait_ge(split_lo, PIECES * (HALVES + b) + p + 1)
                sp.sem_inc(sp_passed, 1)
                sp.dma_start(hi_dram[cols((E - 1 - b) * P, P), p * PIECE:(p + 1) * PIECE], w_hi[:, at].bitcast(F32)
                             ).then_inc(split_dma[p], 16)
                sp.dma_start(lo_dram[cols((E - 1 - b) * P, P), p * PIECE:(p + 1) * PIECE], w_lo[:, at].bitcast(F32)
                             ).then_inc(split_dma[p], 16)

            def batch(b, s, more):
                if more:
                    wait(sp, var2_ready, b)
                    load_x(b + 1, 1 - s)
                    wait(sp, num_ready, b)
                    load_v(b + 1, 1 - s)
                if not isinstance(b, int) or b >= 2:
                    store_base(2 * b - 3, 1, s)
                for p in range(PIECES):
                    if not isinstance(b, int) or b >= 1:
                        store_piece(b - 1, p)
                    load_piece(HALVES + b, p)
                if not isinstance(b, int) or b >= 1:
                    store_base(2 * b - 2, 0, 1 - s)
                sp.wait_ge(xn_ready, b + 1)
                sp.dma_start(xn_dram[cols(b * T, T), :].rearrange("(j p) c -> p j c", p=P),
                             xn[:, :, :]).then_inc(xn_dma, 16)

            load_x(0, 0)
            sp.dma_start(wrow[0:1, :], w_row).then_inc(const_in, 16)
            sp.dma_start(wrow[32:33, :], w_row).then_inc(const_in, 16)
            sp.dma_start(w_ch[:, :], wu_ch[:, 0:CT]).then_inc(const_in, 16)
            sp.dma_start(u_ch[:, :], wu_ch[:, CT:2 * CT]).then_inc(const_in, 16)
            sp.dma_start(bias_sb[:, :], bias).then_inc(const_in, 16)
            load_v(0, 0)
            for p in range(PIECES):
                load_piece(0, p)
            load_x(1, 1)
            load_v(1, 1)
            sp.wait_ge(zeros_ready, 1)
            sp.dma_start(out[B * T:B * T + SPARE_ROWS, :], q_st[:, 0:2, :].rearrange("p a t -> p (a t)")
                         ).then_inc(zero_dma, 16)
            for p in range(PIECES):
                load_piece(1, p)
            batch(0, 0, False)
            batch(1, 1, True)
            with sp.Fori(0, (B - 4) // 2) as i:
                batch(2 * i + 2, 0, True)
                batch(2 * i + 3, 1, True)
            batch(B - 2, 0, True)
            batch(B - 1, 1, False)
            store_base(TILES - 3, 1, 0)
            store_base(TILES - 2, 0, 1)

            sp.wait_ge(split_lo, PIECES * UNITS)
            sp.sem_inc(w_ready, 1)
            for p in range(PIECES):
                sp.wait_ge(split_dma[p], 32 * (E - 1))

            def load_expert(e):
                r = (e + 2) % REGIONS
                for p in range(PIECES):
                    at = piece_at(r, p)
                    rows, part = slice(e * P, (e + 1) * P), slice(p * PIECE, (p + 1) * PIECE)
                    sp.dma_start(w_hi[:, at].bitcast(F32), hi_dram[rows, part]).then_inc(region_dma[p % 2], 16)
                    sp.dma_start(w_lo[:, at].bitcast(F32), lo_dram[rows, part]).then_inc(region_dma[p % 2], 16)
                    if p > 0:
                        sp.wait_ge(region_dma[(p - 1) % 2], 32 * (PIECES // 2 * (e - 1) + (p - 1) // 2 + 1))
                sp.wait_ge(region_dma[1], 32 * PIECES // 2 * e)
                sp.sem_inc(w_ready, 1)

            store_base(TILES - 1, 1, 1)
            for par in range(2):
                sp.wait_ge(xg_dma[par], 16)
            sp.wait_ge(down_done, TILES * HALVES)
            load_expert(1)
            load_expert(2)
            sp.wait_ge(steps_ready, 1)
            for e in range(3, E):
                until = sp.value_load(ends_i[0:1, e - 3:e - 2], min_val=1, max_val=STEPS + 1)
                sp.wait_ge(step_done, until)
                load_expert(e)

        @block.gpsimd
        def _(pool):
            mk = Marks(pool, pool_mk)
            pool.memset(ident[:, :], 0.0)
            pool.memset(neg_w[:, :].bitcast(F32), 0.0)
            pool.memset(ramp[:, :].bitcast(F32), 0.0)
            pool.iota(row_ii[:, :], pattern=[[0, 1]], base=0, channel_multiplier=1)
            mk.need(mk.mark(pool.iota(iota_i[:, :], pattern=[[1, T]], base=0, channel_multiplier=0)))
            pool.affine_select(out=ident[:, :], in_=ident[:, :], compare_op=ALU.not_equal, fill=1.0,
                               base=0, pattern=[[-1, P]], channel_multiplier=1).then_inc(pool_const, 1)
            pool.memset(minus_half[:, :], -0.5)
            pool.memset(h_sb[:, :, :], 0.0)
            mk.need(mk.mark(pool.memset(q_st[:, :, :], 0.0)))
            pool.sem_inc(zeros_ready, 1)

            def rstd_of(n):
                var = moments[:, n, :, 1:2].rearrange("p j o -> p (j o)")
                pool.sem_inc(pool_passed, 1)
                d = mk.mark(pool.tensor_scalar(rstd[:, n, :], var, EPS, None, ALU.add))
                mk.need(d)
                return pool.tensor_tensor(rstd[:, n, :], rstd[:, n, :], minus_half[:, :], ALU.pow)

            def rstd1(b):
                wait(pool, var1_ready, b + 1)
                rstd_of(0).then_inc(rstd1_ready, 1)

            def rstd2(b):
                wait(pool, var2_ready, b + 1)
                rstd_of(1).then_inc(rstd2_ready, 1)

            def numerator(b, s):
                wait(pool, own_ready, b + 1)
                wait(pool, ev_ready, b + 1)
                pool.sem_inc(pool_passed, 1)
                m = mk.mark(pool.tensor_tensor(v_in[:, s, :, :], v_in[:, s, :, :], own[:, :, :], ALU.mult))
                mk.need(m)
                wait(pool, p_ready, b + 1)
                pool.sem_inc(pool_passed, 1)
                pool.tensor_tensor(ev[:, :, :], p_st[:, :, :], v_in[:, s, :, :], ALU.add).then_inc(num_ready, 1)

            def split(unit, region, p):
                n = PIECE0 if region == 0 else PIECE
                at = piece_at(region, p, n)
                pool.wait_ge(split_hi, PIECES * unit + p + 1)
                pool.tensor_tensor(w_lo[:, at], w_raw[:, p, 0:n], w_hi[:, at].bitcast(F32), ALU.subtract
                                   ).then_inc(split_lo, 1)

            def batch(b, s, more):
                numerator(b, s)
                for p in range(PIECES):
                    if p == 3:
                        if more:
                            rstd1(b + 1)
                        rstd2(b)
                    split(HALVES + b - 1, 2, p)

            rstd1(0)
            split(0, 0, 0)
            split(0, 0, 1)
            numerator(0, 0)
            split(0, 0, 2)
            split(0, 0, 3)
            split(1, 1, 0)
            rstd1(1)
            split(1, 1, 1)
            rstd2(0)
            split(1, 1, 2)
            split(1, 1, 3)
            per0 = mk.k
            batch(1, 1, True)
            start2, per = mk.k, mk.k - per0
            with pool.Fori(0, (B - 4) // 2) as i:
                mk.start(start2 + 2 * per * i)
                batch(2 * i + 2, 0, True)
                batch(2 * i + 3, 1, True)
                assert mk.k == 2 * per
            mk.start(start2 + 4 * per)
            batch(B - 2, 0, True)
            batch(B - 1, 1, False)
            for p in range(PIECES):
                split(UNITS - 1, 2, p)

            pool.wait_ge(idx_ready, 1)
            pool.wait_ge(xn_dma, 16 * B)
            pool.wait_ge(zero_dma, 16)

            def gather(s, k, par):
                if not isinstance(s, int) or s >= 2:
                    pool.wait_ge(xg_dma[par], 16 * k)
                pool.tensor_copy(gather_col[:, par:par + 1], idx_tab[:, 0, cols(s, 1)]).then_inc(idx_set, 1)
                pool.wait_ge(idx_set, s + 1)
                wait(pool, b_xt_done, s - 1)
                pool.sem_inc(pool_passed, 1)
                pool.indirect_dma_start(
                    xg[par], None, xn_dram[:, :],
                    bass.IndirectOffsetOnAxis(ap=gather_col[:, par:par + 1].bitcast(U32), axis=0)
                    ).then_inc(xg_dma[par], 16)

            def add(s, par):
                wait(pool, add_dma, 16 * s)
                pool.tensor_copy(add_col[:, par:par + 1], idx_tab[:, 1, cols(s, 1)]).then_inc(add_set, 1)
                pool.wait_ge(add_set, s + 1)
                pool.wait_ge(ys_ready, s + 1)
                pool.sem_inc(pool_passed, 1)
                pool.indirect_dma_start(
                    out[:, :], bass.IndirectOffsetOnAxis(ap=add_col[:, par:par + 1].bitcast(U32), axis=0),
                    ys[par], None, compute_op=ALU.add).then_inc(add_dma, 16)

            gather(0, 0, 0)
            gather(1, 0, 1)
            for par in range(2):
                pool.wait_ge(base_dma[par], 16 * TILES // 2)
            gather(2, 1, 0)
            gather(3, 1, 1)
            add(0, 0)
            with pool.Fori(1, (STEPS - 3) // 2) as i:
                for par in range(2):
                    gather(2 * i + par + 2, i + 1, par)
                    add(2 * i + par - 1, 1 - par)
            gather(STEPS - 1, STEPS // 2, 0)
            add(STEPS - 4, 1)
            add(STEPS - 3, 0)
            add(STEPS - 2, 1)
            add(STEPS - 1, 0)
            pool.wait_ge(add_dma, 16 * STEPS)

        @block.scalar
        def _(act):
            def split(unit, region, p, k):
                n = PIECE0 if region == 0 else PIECE
                at = piece_at(region, p, n)
                act.wait_ge(raw_dma[p], 16 * k)
                if region == 2 and not (isinstance(unit, int) and unit <= HALVES):
                    act.wait_ge(split_dma[p], 32 * (unit - HALVES))
                act.activation(w_hi[:, at], w_raw[:, p, 0:n], ACT.Copy).then_inc(split_hi, 1)

            def part_exp(b):
                wait(act, y_ready, 2 * b)
                key = [ky[:, c // 2, (c % 2) * T:(c % 2) * T + T] for c in range(CT)]
                for h in range(2):
                    wait(act, k_done, 2 * b + h + 1)
                    for c in (2 * h, 2 * h + 1):
                        last = act.activation(e2[:, c, :], key[c], ACT.Exp, bias=state_log[:, c:c + 1])
                    last.then_inc(e2_ready, 1)
                for c in range(CT):
                    last = act.activation(own[:, c, :], key[c], ACT.Exp, bias=own_log[:, c:c + 1])
                last.then_inc(own_ready, 1)

            def unit(n, u, tile=None, between=None):
                par = u % 2
                wait(act, g_done, n + 1)
                wait(act, h_ready, n - 1)
                if tile is not None and u % HALVES == 0:
                    act.activation(score.rearrange("p t e -> p (t e)")[:, cols(tile * E, E)],
                                   g_ps[:, H:H + E], ACT.Copy)
                act.activation(silu_g[:, par, :], g_ps[:, 0:H], ACT.Silu).then_inc(silu_ready, 1)
                if between is not None:
                    split(*between)
                wait(act, ht_done, n + 1)
                wait(act, down_done, n - 1)
                act.activation(h_hi[:, par, :, :].rearrange("p a t -> p (a t)"), ht_ps[:, 0:HC * P], ACT.Copy
                               ).then_inc(hhi_ready, 1)

            def part_x(b, s):
                for j in range(TJ):
                    wait(act, xt_done, 2 * b + j + 1)
                    wait(act, down_done, PER_BATCH * (b - 1))
                    act.activation(x_hi[:, s, j, :, :].rearrange("p a t -> p (a t)"), xt_ps[:, j, :], ACT.Copy
                                   ).then_inc(xhi_ready, 1)

            def batch(b, s):
                part_exp(b)
                if isinstance(b, int) and b == B - 1:
                    act.wait_ge(silu_ready, PER_BATCH * (b - 1))
                    act.activation(score[:, 0:EARLY, :], score[:, 0:EARLY, :], ACT.Exp, scale=-1.0
                                   ).then_inc(score_ready, 1)
                for u in range(PER_BATCH):
                    unit(PER_BATCH * (b - 1) + u, u, 2 * (b - 1) + u // 2,
                         between=(HALVES + b - 1, 2, u, HALVES + b))
                part_x(b, s)

            act.wait_ge(dve_const, 1)
            act.activation(decay[:, :], decay[:, :], ACT.Exp).then_inc(act_mk, 1)
            split(0, 0, 0, 1)
            split(0, 0, 1, 1)
            part_exp(0)
            split(0, 0, 2, 1)
            split(0, 0, 3, 1)
            split(1, 1, 0, 2)
            split(1, 1, 1, 2)
            split(1, 1, 2, 2)
            split(1, 1, 3, 2)
            part_x(0, 0)
            batch(1, 1)
            with act.Fori(0, (B - 4) // 2) as i:
                batch(2 * i + 2, 0)
                batch(2 * i + 3, 1)
            batch(B - 2, 0)
            batch(B - 1, 1)
            act.wait_ge(logit_done, 1)
            act.activation(score.rearrange("p t e -> p (t e)")[:, (TILES - TJ) * E:TILES * E], logit_ps, ACT.Copy
                           ).then_inc(logit_read, 1)
            act.wait_ge(logit_read, 1)
            act.activation(score[:, EARLY:TILES, :], score[:, EARLY:TILES, :], ACT.Exp, scale=-1.0
                           ).then_inc(score_ready, 1)
            for u in range(PER_BATCH):
                unit(PER_BATCH * (B - 1) + u, u, between=(UNITS - 1, 2, u, UNITS))

            def turned(s, par):
                wait(act, b_xt_done, s + 1)
                wait(act, b_u_done, s - 1)
                act.activation(x_hi[:, par, 0, :, :].rearrange("p a t -> p (a t)"), xt_ps[:, par, :], ACT.Copy
                               ).then_inc(b_xhi_ready, 1)

            def gate(s, par):
                wait(act, b_g_done, s + 1)
                wait(act, b_h_ready, s - 1)
                act.activation(silu_g[:, par, :], g_ps[:, 0:H], ACT.Silu).then_inc(b_silu_ready, 1)

            def hidden(s, par):
                wait(act, b_turn_done, s + 1)
                wait(act, step_done, s)
                act.activation(h_hi[:, par, :, :].rearrange("p a t -> p (a t)"), ht_ps[:, 0:HC * P], ACT.Copy
                               ).then_inc(b_hhi_ready, 1)

            def result(s, par):
                wait(act, step_done, s + 2)
                wait(act, add_dma, 16 * (s - 1))
                act.activation(ys[par], d_ps[:, :], ACT.Copy, scale=w_slot[:, cols(s, 1)]).then_inc(ys_ready, 1)

            def pair(i):
                for par in (1, 0):
                    s = 2 * i + 2 - par
                    gate(s, par)
                    turned(s + 1, 1 - par)
                    result(s - 1, 1 - par)
                    hidden(s, par)

            act.wait_ge(idx_ready, 1)
            turned(0, 0)
            gate(0, 0)
            turned(1, 1)
            hidden(0, 0)
            pair(0)
            with act.Fori(1, (STEPS - 3) // 2) as i:
                pair(i)
            gate(STEPS - 2, 1)
            turned(STEPS - 1, 0)
            result(STEPS - 3, 0)
            hidden(STEPS - 2, 1)
            gate(STEPS - 1, 0)
            result(STEPS - 2, 1)
            hidden(STEPS - 1, 0)
            result(STEPS - 1, 0)

        @block.vector
        def _(dve):
            mk = Marks(dve, dve_mk)
            def moments_of(n, src):
                for j in range(TJ):
                    m = mk.mark(dve.bn_stats(stats[:, n, j, :], src[:, j, :]))
                mk.need(m)
                dve.sem_inc(dve_passed, 1)
                for j in range(TJ):
                    last = dve.bn_aggr(moments[:, n, j, :], stats[:, n, j, :])
                return last

            def key_moments(b, k, s):
                wait(dve, x_dma[s], 16 * (k + 1))
                moments_of(0, x_in[:, s]).then_inc(var1_ready, 1)

            def norm(dst, src, n):
                for j in range(TJ):
                    last = dve.tensor_scalar(dst[:, j, :], src[:, j, :], moments[:, n, j, 0:1], rstd[:, n, j:j + 1],
                                             ALU.subtract, ALU.mult)
                return last

            def keys(b, s):
                wait(dve, rstd1_ready, b + 1)
                wait(dve, k_done, 2 * b)
                norm(k_tok, x_in[:, s], 0).then_inc(ktok_ready, 1)

            def unit_h(n, u):
                par = u % 2
                wait(dve, u_done, n + 1)
                wait(dve, silu_ready, n + 1)
                wait(dve, ht_done, n - 1)
                dve.tensor_tensor(h_sb[:, par, 0:H], silu_g[:, par, :], u_ps[:, 0:H], ALU.mult
                                  ).then_inc(h_ready, 1)

            def unit_lo(n, u):
                par = u % 2
                wait(dve, hhi_ready, n + 1)
                dve.tensor_tensor(h_lo[:, par, :, :].rearrange("p a t -> p (a t)"), ht_ps[:, 0:HC * P],
                                  h_hi[:, par, :, :].rearrange("p a t -> p (a t)").bitcast(F32), ALU.subtract
                                  ).then_inc(hlo_ready, 1)

            def unit(n, u):
                unit_h(n, u)
                unit_lo(n, u)

            def add_base(n, j, s):
                wait(dve, down_done, n + 1)
                dve.tensor_tensor(x1[:, s, j, :], x1[:, s, j, :], d_ps[:, :], ALU.add).then_inc(base_ready, 1)

            def inverse(c):
                return dve.reciprocal(e2[:, c, :], q_st[:, c, :])

            def half(buf, h):
                return buf[:, 2 * h:2 * h + 2, :]

            def bc(ap, dim, n):
                shape = list(ap.shape)
                shape.insert(dim, n)
                return ap.unsqueeze(dim).broadcast_to(shape)

            def chain(ins):
                mk.need(mk.mark(ins))

            def scores(t0, t1):
                wait(dve, score_ready, 1 if t0 == 0 else 2)
                part, part_b = score[:, t0:t1, :], biased[:, t0:t1, :]
                chain(dve.tensor_scalar(part, part, 1.0, None, ALU.add))
                chain(dve.reciprocal(part, part))
                chain(dve.tensor_tensor(part_b, part, bc(bias_sb[:, :], 1, t1 - t0), ALU.add))
                for t in range(t0, t1):
                    m = mk.mark(dve.max(top_v[:, t, :], biased[:, t, :]))
                mk.need(m)

            def best(t0, t1):
                for t in range(t0, t1):
                    dve.max_index(top_i[:, t, :], top_v[:, t, :], biased[:, t, :])

            def choose():
                mk.need(mk.mark(dve.memset(ones_b[:, :], 1.0)))
                chain(dve.tensor_copy(top_f[:, :, :], top_i[:, :, 0:TOPK]))
                for k in range(TOPK):
                    m = mk.mark(dve.tensor_tensor(onehot[:, :, k, :], bc(iota_f[:, 0:E], 1, TILES),
                                                  bc(top_f[:, :, k], 2, E), ALU.is_equal))
                mk.need(m)
                chain(dve.tensor_tensor(chosen.rearrange("p e t -> p t e"), onehot[:, :, 0, :],
                                        onehot[:, :, 1, :], ALU.add))
                chain(dve.memset(first0[:, :, :], 1.0))
                chain(dve.memset(first0[:, :, 0:1], 0.0))
                flat = lambda ap: ap.rearrange("p e t -> p (e t)")
                dve.tensor_copy(chosen_b[:, :], flat(chosen[:, :, :]))
                chain(dve.tensor_tensor_scan(flat(upto[:, :, :]), flat(first0[:, :, :]), flat(chosen[:, :, :]),
                                             0.0, ALU.mult, ALU.add))
                dve.tensor_copy(total_b[:, :], upto[:, :, TILES - 1])
                dve.tensor_copy(row_id[:, :], row_ii[:, :])
                dve.tensor_scalar(row_id1[:, :], row_ii[:, :], 1.0, None, ALU.add)
                dve.tensor_scalar(dump, row_ii[:, :], float(B * T + 1), None, ALU.add)
                chain(dve.tensor_tensor(before_b[:, :], flat(upto[:, :, :]), flat(chosen[:, :, :]), ALU.subtract))
                dve.tensor_scalar(tri[:, :], iota_f[:, 0:P], row_id[:, 0:1], None, ALU.is_gt
                                  ).then_inc(chosen_ready, 1)

            def gates():
                for k in range(TOPK):
                    m = mk.mark(dve.tensor_tensor(picked[:, :, k, :], onehot[:, :, k, :], score[:, :, :], ALU.mult))
                mk.need(m)
                chain(dve.reduce_sum(w_top[:, :, :], picked[:, :, :, :], AX.X))
                chain(dve.tensor_tensor(w_sum[:, :], w_top[:, :, 0], w_top[:, :, 1], ALU.add))
                chain(dve.reciprocal(w_sum[:, :], w_sum[:, :]))
                dve.tensor_tensor(w_tok[:, :, :], w_top[:, :, :], bc(w_sum[:, :], 2, TOPK), ALU.mult)
                dve.tensor_scalar(token_id[:, :, :], bc(iota_f[:, 0:TILES], 2, TOPK), float(P),
                                  row_id1[:, 0:1], ALU.mult, ALU.add)

            def places():
                dve.wait_ge(rank_done, 1)
                chain(dve.tensor_scalar(n_i[:, :], count_ps, float(P - 1), float(P), ALU.add, ALU.max))
                chain(dve.tensor_scalar(n_i[:, :], n_i[:, :], 7, None, ALU.logical_shift_right))
                chain(dve.tensor_copy(n_tiles[:, :], n_i[:, :]))
                chain(dve.tensor_tensor_scan(ends[:, :], ones8[:, :], n_tiles[:, :], 0.0, ALU.mult, ALU.add))
                chain(dve.tensor_tensor(starts[:, :], ends[:, :], n_tiles[:, :], ALU.subtract))
                chain(dve.scalar_tensor_tensor(place[:, :, :], bc(starts[:, :], 2, TILES), float(P),
                                               rank_ps.rearrange("p (e t) -> p e t", e=E), ALU.mult, ALU.add))
                for k in range(TOPK):
                    m = mk.mark(dve.tensor_tensor(picked[:, :, k, :], onehot[:, :, k, :],
                                                  place.rearrange("p e t -> p t e"), ALU.mult))
                mk.need(m)
                chain(dve.reduce_sum(slot_f[:, :, :], picked[:, :, :, :], AX.X))
                chain(dve.tensor_copy(slot_i[:, :, :], slot_f[:, :, :]))
                dve.tensor_scalar(part_i[:, 0, :, :], slot_i[:, :, :], P - 1, None, ALU.bitwise_and)
                chain(dve.tensor_scalar(part_i[:, 1, :, :], slot_i[:, :, :], 7, None, ALU.logical_shift_right))
                chain(dve.tensor_copy(part_f[:, :, :, :], part_i[:, :, :, :]))

            def tables(g):
                at = [ap.rearrange("p t k -> p (t k)")[:, g * GROUP:(g + 1) * GROUP]
                      for ap in (part_f[:, 0], part_f[:, 1], token_id[:, :, :], w_tok[:, :, :])]
                wait(dve, onehot_used, g - 2)
                m = mk.mark(dve.tensor_tensor(is_step[:, g % 2, :, :], bc(iota_f[:, 0:STEPS_PAD], 1, GROUP),
                                              bc(at[1], 2, STEPS_PAD), ALU.is_equal))
                dve.tensor_tensor(at_row[g % 3], bc(iota_f[:, 0:P], 1, GROUP), bc(at[0], 2, P),
                                  ALU.is_equal)
                mk.need(m)
                for a in range(2):
                    last = dve.tensor_tensor(at_step[g % 3][:, :, a, :], is_step[:, g % 2, :, :],
                                             bc(at[2 + a], 2, STEPS_PAD), ALU.mult)
                last.then_inc(onehot_ready, 1)

            def steps():
                chain(dve.tensor_tensor(past[:, :, :], bc(iota_f[:, 0:STEPS_PAD], 1, E - 1),
                                        bc(ends[:, 0:E - 1], 2, STEPS_PAD), ALU.is_ge))
                chain(dve.reduce_sum(of_step[:, :], past.rearrange("p e s -> p s e"), AX.X))
                dve.tensor_scalar(w_need[:, :], of_step[:, :], 1.0, None, ALU.add)
                chain(dve.tensor_scalar(w_off_f[:, :], of_step[:, :], float(HALVES), None, ALU.add))
                for e in range(0, E - 1, 3):
                    chain(dve.scalar_tensor_tensor(w_off_f[:, :], past[:, e, :], -3.0, w_off_f[:, :],
                                                   ALU.mult, ALU.add))
                chain(dve.tensor_scalar(slot_no, w_off_f[:, :], 0.5, float(WCOLS0 - WCOLS), ALU.is_gt, ALU.mult))
                dve.scalar_tensor_tensor(w_off[:, :], w_off_f[:, :], float(WCOLS), slot_no, ALU.mult, ALU.add)
                chain(dve.tensor_scalar(ends_i[:, :], ends[:, :], 1.0, None, ALU.add))
                dve.nop().then_inc(steps_ready, 1)

            def slots():
                dve.wait_ge(onehot_used, GROUPS)
                chain(dve.tensor_copy(slot_v, table_ps[:, 0:STEPS_PAD]))
                dve.tensor_copy(w_slot[:, :], table_ps[:, STEPS_PAD:2 * STEPS_PAD])
                dve.tensor_scalar(idx_tab[:, 0, :], slot_v, -1.0, 0.0, ALU.add, ALU.max)
                chain(dve.tensor_scalar(slot_no, slot_v, 0.0, dump, ALU.is_equal, ALU.mult))
                dve.scalar_tensor_tensor(idx_tab[:, 1, :], slot_v, -1.0, slot_no, ALU.add, ALU.add
                                         ).then_inc(idx_ready, 1)

            def batch(b, k, s, units, more):
                n0 = PER_BATCH * (b - 1)
                wait(dve, v_dma[s], 16 * (k + 1))
                dve.tensor_copy(p_st[:, :, 0:1], v_in[:, s, :, 0:1])
                for h in range(2):
                    wait(dve, e2_ready, 2 * b + h + 1)
                    m_ev = mk.mark(dve.tensor_tensor(half(ev, h), half(e2, h), v_in[:, s, 2 * h:2 * h + 2, :],
                                                     ALU.mult))
                mk.need(m_ev)
                dve.sem_inc(ev_ready, 1)
                if isinstance(b, int) and b == 0:
                    dve.wait_ge(zero_dma, 16)
                dve.memset(q_st[:, :, 0:1], 1.0)
                wait(dve, num_ready, b)
                for c in range(CT):
                    scan = dve.tensor_tensor_scan(p_st[:, c, 1:T], decay[:, c:c + 1].broadcast_to([P, T - 1]),
                                                  ev[:, c, 0:T - 1], 0.0, ALU.mult, ALU.add)
                scan.then_inc(p_ready, 1)
                for c in range(CT):
                    m_scan = mk.mark(dve.tensor_tensor_scan(
                        q_st[:, c, 1:T], decay[:, c:c + 1].broadcast_to([P, T - 1]),
                        e2[:, c, 0:T - 1], 0.0, ALU.mult, ALU.add))
                if units:
                    unit_h(n0, 0)
                wait(dve, own_ready, b + 1)
                mk.need(m_scan)
                for h in range(2):
                    m_den = mk.mark(dve.tensor_tensor(half(q_st, h), half(q_st, h), half(own, h), ALU.add))
                if units:
                    unit_lo(n0, 0)
                    if not isinstance(b, int) or b >= 2:
                        add_base(n0 - 1, 1, s)
                mk.need(m_den)
                inverse(0)
                inverse(1)
                if units:
                    unit_h(n0 + 1, 1)
                inverse(2)
                if units:
                    unit_lo(n0 + 1, 1)
                m_rec = mk.mark(inverse(3))
                wait(dve, num_ready, b + 1)
                mk.need(m_rec)
                for h in range(2):
                    dve.tensor_tensor(half(ev, h), half(ev, h), half(e2, h), ALU.mult).then_inc(y_ready, 1)
                if units:
                    unit_h(n0 + 2, 2)
                if more:
                    key_moments(b + 1, k if s == 0 else k + 1, 1 - s)
                if not more:
                    scores(0, EARLY)
                if units:
                    add_base(n0 + 1, 0, 1 - s)
                wait(dve, y_done, b + 1)
                if not isinstance(b, int) or b >= 2:
                    dve.wait_ge(base_dma[s], 32 * k)
                m_x1 = mk.mark(dve.tensor_tensor(x1[:, s, :, :], x_in[:, s, :, :], ky[:, :, :], ALU.add))
                mk.need(m_x1)
                dve.sem_inc(x1_ready, 1)
                if units:
                    unit_lo(n0 + 2, 2)
                moments_of(1, x1[:, s]).then_inc(var2_ready, 1)
                if more:
                    keys(b + 1, 1 - s)
                if not more:
                    best(0, EARLY)
                if units:
                    unit_h(n0 + 3, 3)
                wait(dve, rstd2_ready, b + 1)
                wait(dve, xn_dma, 16 * b)
                wait(dve, xt_done, 2 * b)
                norm(xn, x1[:, s], 1).then_inc(xn_ready, 1)
                if units:
                    unit_lo(n0 + 3, 3)
                for j in range(TJ):
                    wait(dve, xhi_ready, 2 * b + j + 1)
                    dve.tensor_tensor(x_lo[:, s, j, :, :].rearrange("p a t -> p (a t)"), xt_ps[:, j, :],
                                      x_hi[:, s, j, :, :].rearrange("p a t -> p (a t)").bitcast(F32),
                                      ALU.subtract).then_inc(xlo_ready, 1)

            key_moments(0, 0, 0)
            dve.wait_ge(const_in, 16 * N_CONST)
            a = mk.mark(dve.tensor_scalar(lift[:, :], w_ch[:, :], 0.0, None, ALU.max))
            dve.tensor_scalar(decay[:, :], w_ch[:, :], 0.0, None, ALU.min)
            mk.need(a)
            a = mk.mark(dve.tensor_tensor(lift[:, :], lift[:, :], u_ch[:, :], ALU.add))
            mk.need(a)
            dve.tensor_scalar(own_log[:, :], lift[:, :], 0.0, None, ALU.min)
            dve.tensor_scalar(state_log[:, :], lift[:, :], 0.0, -1.0, ALU.max, ALU.mult).then_inc(dve_const, 1)
            dve.wait_ge(pool_const, 1)
            for row in (0, 32):
                c1 = mk.mark(dve.tensor_scalar(wrow[row:row + 1, :], wrow[row:row + 1, :], -1.0, 0.0,
                                               ALU.mult, ALU.min))
            mk.need(c1)
            for row in (0, 32):
                c2 = mk.mark(dve.tensor_copy(neg_w[row:row + 1, :], wrow[row:row + 1, :]))
            mk.need(c2)
            dve.tensor_tensor(neg_w[32:33, :], wrow[32:33, :], neg_w[32:33, :].bitcast(F32), ALU.subtract)
            for row in (0, 32):
                dve.tensor_copy(ramp[row:row + 1, :], iota_i[row:row + 1, :])
            mk.mark(dve.tensor_copy(iota_f[:, :], iota_i[:, :]))
            dve.memset(ones8[:, :], 1.0).then_inc(dve_const, 1)
            keys(0, 0)
            dve.wait_ge(act_mk, 1)
            batch(0, 0, 0, False, True)
            per0 = mk.k
            batch(1, 0, 1, True, True)
            start2, per = mk.k, mk.k - per0
            with dve.Fori(0, (B - 4) // 2) as i:
                mk.start(start2 + 2 * per * i)
                batch(2 * i + 2, i + 1, 0, True, True)
                batch(2 * i + 3, i + 1, 1, True, True)
                assert mk.k == 2 * per
            mk.start(start2 + 4 * per)
            batch(B - 2, B // 2 - 1, 0, True, True)
            batch(B - 1, B // 2 - 1, 1, True, False)

            n7 = PER_BATCH * (B - 1)
            unit(n7, 0)
            add_base(n7 - 1, 1, 0)
            scores(EARLY, TILES)
            best(EARLY, TILES)
            choose()
            unit_h(n7 + 1, 1)
            gates()
            unit_lo(n7 + 1, 1)
            places()
            unit_h(n7 + 2, 2)
            tables(0)
            unit_lo(n7 + 2, 2)
            add_base(n7 + 1, 0, 1)
            tables(1)
            tables(2)
            unit_h(n7 + 3, 3)
            tables(3)
            unit_lo(n7 + 3, 3)
            steps()
            slots()
            add_base(n7 + 3, 1, 1)

            def turned(s, par):
                wait(dve, b_xhi_ready, s + 1)
                dve.tensor_tensor(x_lo[:, par, 0, :, :].rearrange("p a t -> p (a t)"), xt_ps[:, par, :],
                                  x_hi[:, par, 0, :, :].rearrange("p a t -> p (a t)").bitcast(F32),
                                  ALU.subtract).then_inc(b_xlo_ready, 1)

            def hidden(s, par):
                wait(dve, b_u_done, s + 1)
                wait(dve, b_silu_ready, s + 1)
                wait(dve, b_turn_done, s - 1)
                dve.tensor_tensor(h_sb[:, par, 0:H], silu_g[:, par, :], u_ps[:, 0:H], ALU.mult
                                  ).then_inc(b_h_ready, 1)

            def hidden_lo(s, par):
                wait(dve, b_hhi_ready, s + 1)
                dve.tensor_tensor(h_lo[:, par, :, :].rearrange("p a t -> p (a t)"), ht_ps[:, 0:HC * P],
                                  h_hi[:, par, :, :].rearrange("p a t -> p (a t)").bitcast(F32), ALU.subtract
                                  ).then_inc(b_hlo_ready, 1)

            def step(s, par, more):
                hidden(s, par)
                if more:
                    turned(s + 1, 1 - par)
                hidden_lo(s, par)

            turned(0, 0)
            step(0, 0, True)
            step(1, 1, True)
            step(2, 0, True)
            with dve.Fori(1, (STEPS - 3) // 2) as i:
                step(2 * i + 1, 1, True)
                step(2 * i + 2, 0, True)
            step(STEPS - 2, 1, True)
            step(STEPS - 1, 0, False)

        @block.tensor
        def _(pe):
            def keys(b, halves):
                wait(pe, ktok_ready, b + 1)
                wait(pe, x1_ready, b)
                for h in halves:
                    for c in (2 * h, 2 * h + 1):
                        region = ky[:, h, (c % 2) * T:(c % 2) * T + T]
                        pe.matmul(region, neg_w[:, c * P:(c + 1) * P], ramp[:, :], start=True, stop=False)
                        for j in range(TJ):
                            last = pe.matmul(region[:, j * P:(j + 1) * P], k_tok[:, j, c * P:(c + 1) * P],
                                             ident[:, :], start=False, stop=(j == TJ - 1))
                    last.then_inc(k_done, 1)

            def y_turn(b):
                for h in range(2):
                    wait(pe, y_ready, 2 * b + h + 1)
                    for j in range(TJ):
                        for c in (2 * h, 2 * h + 1):
                            last = pe.transpose(ky[:, j, c * P:(c + 1) * P], ev[:, c, j * P:(j + 1) * P],
                                                ident[:, :])
                last.then_inc(y_done, 1)

            def x_turn(b):
                wait(pe, xn_ready, b + 1)
                wait(pe, xlo_ready, 2 * b)
                for j in range(TJ):
                    for c in range(CT):
                        last = pe.transpose(xt_ps[:, j, c * P:(c + 1) * P], xn[:, j, c * P:(c + 1) * P],
                                            ident[:, :])
                    last.then_inc(xt_done, 1)

            def product(dst, pairs, first=True, final=True):
                n = len(pairs)
                for i, (a_hi, a_lo, b_hi, b_lo) in enumerate(pairs):
                    pe.matmul(dst, a_hi, b_hi, start=(first and i == 0), stop=False)
                    pe.matmul(dst, a_hi, b_lo, start=False, stop=False)
                    last = pe.matmul(dst, a_lo, b_hi, start=False, stop=(final and i == n - 1))
                return last

            def logits(b, s):
                wait(pe, xlo_ready, 2 * b + 2)
                wait(pe, hlo_ready, PER_BATCH * b)
                at = [slice(c * UP0 + H, c * UP0 + H + E) for c in range(CT)]
                for j in range(TJ):
                    last = product(logit_ps[:, j * E:(j + 1) * E],
                                   [(x_hi[:, s, j, c, :], x_lo[:, s, j, c, :], w_hi[:, at[c]], w_lo[:, at[c]])
                                    for c in range(CT)])
                last.then_inc(logit_done, 1)

            def unit(n, u, s, t0, down_before=True):
                j, half, par = u // HALVES, u % HALVES, u % 2
                if isinstance(n, int) and n == 1:
                    pe.wait_ge(split_lo, PIECES * HALVES)
                if u == 0:
                    wait(pe, xlo_ready, t0 + TJ)
                wait(pe, silu_ready, n)
                width = UP0 if half == 0 else UP
                at = REGION_AT[half]
                for bank, off, n_cols, done in ((g_ps, 0, width - H, g_done), (u_ps, width - H, H, u_done)):
                    if bank is u_ps:
                        wait(pe, h_ready, n)
                    part = [slice(at + c * width + off, at + c * width + off + n_cols) for c in range(CT)]
                    product(bank[:, 0:n_cols],
                            [(x_hi[:, s, j, c, :], x_lo[:, s, j, c, :], w_hi[:, part[c]], w_lo[:, part[c]])
                             for c in range(CT)]).then_inc(done, 1)
                if down_before:
                    down(n - 1, (u - 1) % HALVES, t0 + (u - 1) // HALVES)
                if isinstance(n, int) and n == PER_BATCH * (B - 1):
                    pe.wait_ge(logit_read, 1)
                wait(pe, h_ready, n + 1)
                for c in range(HC):
                    last = pe.transpose(ht_ps[:, c * P:(c + 1) * P], h_sb[:, par, c * P:(c + 1) * P], ident[:, :])
                last.then_inc(ht_done, 1)

            def down(n, half, tile):
                wait(pe, hlo_ready, n + 1)
                if half == 0:
                    wait(pe, base_ready, tile)
                at = REGION_AT[half] + CT * (UP0 if half == 0 else UP)
                part = [slice(at + c * C, at + (c + 1) * C) for c in range(HC)]
                product(d_ps[:, :],
                        [(h_hi[:, half, c, :], h_lo[:, half, c, :], w_hi[:, part[c]], w_lo[:, part[c]])
                         for c in range(HC)],
                        first=(half == 0), final=(half == 1)).then_inc(down_done, 1)

            def batch(b, s, units, more):
                n0 = PER_BATCH * (b - 1)
                for u in range(PER_BATCH if units else 0):
                    if u == 3:
                        y_turn(b)
                    unit(n0 + u, u, 1 - s, TJ * (b - 1), down_before=not (isinstance(b, int) and b == 1 and u == 0))
                if not units:
                    y_turn(b)
                x_turn(b)
                if more:
                    keys(b + 1, (0, 1))
                else:
                    logits(b, s)

            pe.wait_ge(pool_const, 1)
            pe.wait_ge(zeros_ready, 1)
            pe.wait_ge(dve_const, 2)
            keys(0, (0, 1))
            batch(0, 0, False, True)
            pe.wait_ge(split_lo, PIECES)
            batch(1, 1, True, True)
            with pe.Fori(0, (B - 4) // 2) as i:
                batch(2 * i + 2, 0, True, True)
                batch(2 * i + 3, 1, True, True)
            batch(B - 2, 0, True, True)
            batch(B - 1, 1, True, False)

            def table(g):
                pe.wait_ge(onehot_ready, g + 1)
                for n in range(GROUP):
                    last = pe.matmul(table_ps, at_row[g % 3][:, n, :],
                                     at_step[g % 3][:, n, :, :].rearrange("p a s -> p (a s)"),
                                     start=(g == 0 and n == 0), stop=(g == GROUPS - 1 and n == GROUP - 1))
                last.then_inc(onehot_used, 1)

            n7 = PER_BATCH * (B - 1)
            for u in range(PER_BATCH):
                unit(n7 + u, u, 1, TJ * (B - 1))
                if u == 1:
                    pe.wait_ge(chosen_ready, 1)
                    pe.matmul(rank_ps, tri[:, :], chosen_b[:, :], start=True, stop=False)
                    pe.matmul(rank_ps, ones_b[:, :], before_b[:, :], start=False, stop=True)
                    pe.matmul(count_ps, ones_b[:, :], total_b[:, :], start=True, stop=True
                              ).then_inc(rank_done, 1)
                if u == 2:
                    table(0)
            table(1)
            table(2)
            table(3)
            down(n7 + PER_BATCH - 1, 1, TILES - 1)

            def turn_x(s, k, par):
                wait(pe, xg_dma[par], 16 * (k + 1))
                wait(pe, b_xlo_ready, s - 1)
                for c in range(CT):
                    last = pe.transpose(xt_ps[:, par, c * P:(c + 1) * P], xg[par][:, c * P:(c + 1) * P],
                                        ident[:, :])
                last.then_inc(b_xt_done, 1)

            def region_of(s):
                return pe.value_load(w_off[0:1, cols(s, 1)], min_val=0, max_val=REGION_AT[2])

            def up(s, par):
                need = pe.value_load(w_need[0:1, cols(s, 1)], min_val=1, max_val=E)
                off = region_of(s)
                pe.wait_ge(w_ready, need)
                wait(pe, b_xlo_ready, s + 1)
                wait(pe, b_silu_ready, s)
                for bank, o, done in ((g_ps, 0, b_g_done), (u_ps, H, b_u_done)):
                    if bank is u_ps:
                        wait(pe, b_h_ready, s)
                    product(bank[:, 0:H],
                            [(x_hi[:, par, 0, c, :], x_lo[:, par, 0, c, :],
                              w_hi[:, bass.DynSlice(off + (c * UP + o), H)],
                              w_lo[:, bass.DynSlice(off + (c * UP + o), H)]) for c in range(CT)]
                            ).then_inc(done, 1)
                return off

            def down_step(s, par, off):
                wait(pe, b_hlo_ready, s + 1)
                wait(pe, ys_ready, s)
                product(d_ps[:, :],
                        [(h_hi[:, par, c, :], h_lo[:, par, c, :],
                          w_hi[:, bass.DynSlice(off + (DOWN0 + c * C), C)],
                          w_lo[:, bass.DynSlice(off + (DOWN0 + c * C), C)]) for c in range(HC)]
                        ).then_inc(step_done, 1)

            def turn_h(s, par):
                wait(pe, b_h_ready, s + 1)
                wait(pe, b_hlo_ready, s)
                for c in range(HC):
                    last = pe.transpose(ht_ps[:, c * P:(c + 1) * P], h_sb[:, par, c * P:(c + 1) * P], ident[:, :])
                last.then_inc(b_turn_done, 1)

            pe.wait_ge(steps_ready, 1)
            pe.wait_ge(idx_ready, 1)
            pe.wait_ge(base_ready, TILES)
            pe.nop().then_inc(step_done, 1)
            turn_x(0, 0, 0)
            up(0, 0)
            turn_x(1, 0, 1)
            turn_h(0, 0)

            def pair(i):
                s = 2 * i + 1
                off = up(s, 1)
                turn_x(s + 1, i + 1, 0)
                down_step(s - 1, 0, region_of(s - 1))
                turn_h(s, 1)
                up(s + 1, 0)
                turn_x(s + 2, i + 1, 1)
                down_step(s, 1, off)
                turn_h(s + 1, 0)

            pair(0)
            pair(1)
            with pe.Fori(1, (STEPS - 3) // 4) as i:
                pair(2 * i)
                pair(2 * i + 1)
            off = up(STEPS - 2, 1)
            turn_x(STEPS - 1, (STEPS - 1) // 2, 0)
            down_step(STEPS - 3, 0, region_of(STEPS - 3))
            turn_h(STEPS - 2, 1)
            last_off = up(STEPS - 1, 0)
            down_step(STEPS - 2, 1, off)
            turn_h(STEPS - 1, 0)
            down_step(STEPS - 1, 0, last_off)


def kernel(**inputs):
    import numpy as np
    from concourse import bacc
    from concourse import mybir as mb
    from concourse.bass_utils import run_bass_kernel_spmd as run

    a = {k: np.asarray(v) for k, v in inputs.items()}
    hs = HALVES * H

    def unit(up, down):
        w = np.zeros((P, WCOLS0), np.float32)
        n = CT * up.shape[0]
        w[:, :n] = up.T.reshape(CT, P, up.shape[0]).transpose(1, 0, 2).reshape(P, n)
        d = np.zeros((HC * P, C), np.float32)
        d[:H] = down.T
        w[:, n:n + HC * C] = d.reshape(HC, P, C).transpose(1, 0, 2).reshape(P, HC * C)
        return w

    sg, sd = a["L0_ffn_shared_gw"], a["L0_ffn_shared_dw"]
    router = [a["L0_ffn_gate_w"], a["L0_ffn_gate_w"][:0]]
    units = [unit(np.concatenate([sg[hs + h * H:hs + (h + 1) * H], router[h], sg[h * H:(h + 1) * H]]),
                  sd[:, h * H:(h + 1) * H]) for h in range(HALVES)]
    units += [unit(a["L0_ffn_up_w"][e], a["L0_ffn_down_w"][e]) for e in reversed(range(E))]
    arrays = {
        "x_in_dram": np.ascontiguousarray(a["x"]).reshape(B * T, C),
        "ctx_t_dram": np.ascontiguousarray(a["ctx_2048"].transpose(0, 2, 1)).reshape(B * C, T),
        "w_row_dram": np.ascontiguousarray(a["L0_xattn_w"]).reshape(1, C),
        "wu_ch_dram": np.concatenate([a[n].reshape(CT, P).T for n in ("L0_xattn_w", "L0_xattn_u")], axis=1),
        "bias_dram": np.ascontiguousarray(np.broadcast_to(a["L0_ffn_gate_bias"], (P, E))),
        "weights_dram": np.concatenate(units),
    }
    nc = bacc.Bacc("TRN2", target_bir_lowering=False, num_devices=1)
    args = [nc.dram_tensor(n, v.shape, mb.dt.float32, kind="ExternalInput").ap() for n, v in arrays.items()]
    args.append(nc.dram_tensor("xn_scratch", (B * T, C), mb.dt.float32).ap())
    for part in ("hi", "lo"):
        args.append(nc.dram_tensor(f"w_{part}_scratch", (E * P, WCOLS), mb.dt.float32).ap())
    args.append(nc.dram_tensor("out_dram", (B * T + SPARE_ROWS, C), mb.dt.float32, kind="ExternalOutput").ap())
    build(nc, *args)
    r = run(nc, [arrays], core_ids=[0])
    return r.results[0]["out_dram"][:B * T].reshape(B, T, C)
```
